# Optimizing a Trainium2 kernel written in Bass

```python
import numpy as np
import jax
import jax.numpy as jnp

def _softmax(x, axis=-1):
    return jax.nn.softmax(x, axis=axis)
def _gelu(x):
    return jax.nn.gelu(x, approximate=True)
def _silu(x):
    return jax.nn.silu(x)
def _sigmoid(x):
    return jax.nn.sigmoid(x)
def _layernorm(x, axis=-1, eps=1e-5):
    m = jnp.mean(x, axis=axis, keepdims=True)
    v = jnp.var(x, axis=axis, keepdims=True)
    return (x - m) / jnp.sqrt(v + eps)
def _scatter_add(tgt, idx, src, axis=0):
    return tgt.at[idx].add(src)
def _segment_sum(src, seg, n):
    return jax.ops.segment_sum(src, seg, n)

kernel_name = 'mk_conv_preact_d2_conv_nchw192_d55021'

def setup_inputs(seed: int = 0):
    np.random.seed(seed)
    _w = jnp.asarray
    def _rec_inputs():
        import jax
        import jax.numpy as jnp
        _gk = jax.random.key(seed)
        x = -0.0004039 + 1 * jax.random.normal(jax.random.fold_in(_gk, 1), (4, 192, 128, 128), jnp.float32)
        return x
    x = _rec_inputs()
    def _L0_conv_setup():
        import jax, jax.numpy as jnp
        import numpy as np
        from jax import lax
        B, DIM, H, W = (4, 192, 128, 128)
        HEADS = 4

        def _conv3d(x, w, groups=1, pad=0):
            return lax.conv_general_dilated(x, w, (1, 1, 1), [(pad, pad)] * 3, dimension_numbers=('NCDHW', 'OIDHW', 'NCDHW'), feature_group_count=groups)

        def _l2norm(x, eps=1e-12):
            nrm = jnp.sqrt(jnp.sum(x * x, axis=-1, keepdims=True))
            return x / jnp.maximum(nrm, eps)
        key = jax.random.key(seed)
        ks = jax.random.split(key, 13)
        c = DIM
        n = lambda k, s, sc=0.02: jax.random.normal(k, s, jnp.float32) * sc
        return {'x': jax.random.normal(ks[0], (B, c, H, W), jnp.float32), 'temperature': jnp.ones((HEADS, 1, 1), jnp.float32), 'qkv_w': n(ks[1], (3 * c, c, 1, 1, 1)), 'qkv_dw_w': n(ks[2], (3 * c, 1, 3, 3, 3)), 'proj_w': n(ks[3], (c, c, 1, 1, 1)), 'fc_w': n(ks[4], (9, 3 * HEADS, 1, 1, 1)), 'fc_b': n(ks[5], (9,)), 'dep_w': n(ks[6], (c, 9, 3, 3, 3)), 'dep_b': n(ks[7], (c,)), 'gate_w1': n(ks[8], (c // 2, c, 1, 1)), 'gate_b1': n(ks[9], (c // 2,)), 'gate_w2': n(ks[10], (1, c // 2, 1, 1)), 'gate_b2': n(ks[11], (1,))}
    _L0_conv_all = _L0_conv_setup()
    _L0_conv_in = {k: v for k, v in _L0_conv_all.items() if k in ('temperature', 'qkv_w', 'qkv_dw_w', 'proj_w', 'fc_w', 'fc_b', 'dep_w', 'dep_b', 'gate_w1', 'gate_b1', 'gate_w2', 'gate_b2', )}
    del _L0_conv_all

    def _L1_conv_setup():
        import jax, jax.numpy as jnp
        import numpy as np
        LN_EPS = 1e-05
        NEG_INF = -1e+38

        def wkv_scan(w, u, k, v):
            Bdim, T, C = k.shape

            def step(carry, kv_t):
                p, q, o = carry
                kt, vt = kv_t
                no = jnp.maximum(o, u + kt)
                A = jnp.exp(o - no)
                Bw = jnp.exp(u + kt - no)
                y = (A * p + Bw * vt) / (A * q + Bw)
                no2 = jnp.maximum(w + o, kt)
                A2 = jnp.exp(w + o - no2)
                B2 = jnp.exp(kt - no2)
                return ((A2 * p + B2 * vt, A2 * q + B2, no2), y)
            init = (jnp.zeros((Bdim, C), k.dtype), jnp.zeros((Bdim, C), k.dtype), jnp.full((Bdim, C), NEG_INF, k.dtype))
            kT = jnp.moveaxis(k, 1, 0)
            vT = jnp.moveaxis(v, 1, 0)
            _, ys = jax.lax.scan(step, init, (kT, vT))
            return jnp.moveaxis(ys, 0, 1)
        key = jax.random.key(seed)
        ks = jax.random.split(key, 8)
        B, C, H, W = (16, 192, 56, 56)
        s = 0.02
        x = jax.random.normal(ks[0], (B, C, H, W), jnp.float32)
        Wk = jax.random.normal(ks[1], (C, C), jnp.float32) * s
        Wv = jax.random.normal(ks[2], (C, C), jnp.float32) * s
        Wr = jax.random.normal(ks[3], (C, C), jnp.float32) * s
        Wo = jax.random.normal(ks[4], (C, C), jnp.float32) * s
        ln_g = jnp.ones((C,), jnp.float32)
        ln_b = jnp.zeros((C,), jnp.float32)
        w_decay = -6.0 + 0.1 * jax.random.normal(ks[5], (C,), jnp.float32)
        u = 0.1 * jax.random.normal(ks[6], (C,), jnp.float32)
        return {'x': x, 'Wk': Wk, 'Wv': Wv, 'Wr': Wr, 'Wo': Wo, 'ln_g': ln_g, 'ln_b': ln_b, 'w_decay': w_decay, 'u': u}
    _L1_conv_all = _L1_conv_setup()
    _L1_conv_in = {k: v for k, v in _L1_conv_all.items() if k in ('Wk', 'Wv', 'Wr', 'Wo', 'ln_g', 'ln_b', 'w_decay', 'u', )}
    del _L1_conv_all

    return {
        "x": x,
        "L0_conv_temperature": _L0_conv_in["temperature"],
        "L0_conv_qkv_w": _L0_conv_in["qkv_w"],
        "L0_conv_qkv_dw_w": _L0_conv_in["qkv_dw_w"],
        "L0_conv_proj_w": _L0_conv_in["proj_w"],
        "L0_conv_fc_w": _L0_conv_in["fc_w"],
        "L0_conv_fc_b": _L0_conv_in["fc_b"],
        "L0_conv_dep_w": _L0_conv_in["dep_w"],
        "L0_conv_dep_b": _L0_conv_in["dep_b"],
        "L0_conv_gate_w1": _L0_conv_in["gate_w1"],
        "L0_conv_gate_b1": _L0_conv_in["gate_b1"],
        "L0_conv_gate_w2": _L0_conv_in["gate_w2"],
        "L0_conv_gate_b2": _L0_conv_in["gate_b2"],
        "L1_conv_Wk": _L1_conv_in["Wk"],
        "L1_conv_Wv": _L1_conv_in["Wv"],
        "L1_conv_Wr": _L1_conv_in["Wr"],
        "L1_conv_Wo": _L1_conv_in["Wo"],
        "L1_conv_ln_g": _L1_conv_in["ln_g"],
        "L1_conv_ln_b": _L1_conv_in["ln_b"],
        "L1_conv_w_decay": _L1_conv_in["w_decay"],
        "L1_conv_u": _L1_conv_in["u"],
    }

def reference(x, L0_conv_temperature, L0_conv_qkv_w, L0_conv_qkv_dw_w, L0_conv_proj_w, L0_conv_fc_w, L0_conv_fc_b, L0_conv_dep_w, L0_conv_dep_b, L0_conv_gate_w1, L0_conv_gate_b1, L0_conv_gate_w2, L0_conv_gate_b2, L1_conv_Wk, L1_conv_Wv, L1_conv_Wr, L1_conv_Wo, L1_conv_ln_g, L1_conv_ln_b, L1_conv_w_decay, L1_conv_u):
    import jax
    import jax.numpy as jnp
    def _L0_conv_ref(x, temperature, qkv_w, qkv_dw_w, proj_w, fc_w, fc_b, dep_w, dep_b, gate_w1, gate_b1, gate_w2, gate_b2):
        import jax, jax.numpy as jnp
        import numpy as np
        from jax import lax
        B, DIM, H, W = (4, 192, 128, 128)
        HEADS = 4

        def _conv3d(x, w, groups=1, pad=0):
            return lax.conv_general_dilated(x, w, (1, 1, 1), [(pad, pad)] * 3, dimension_numbers=('NCDHW', 'OIDHW', 'NCDHW'), feature_group_count=groups)

        def _l2norm(x, eps=1e-12):
            nrm = jnp.sqrt(jnp.sum(x * x, axis=-1, keepdims=True))
            return x / jnp.maximum(nrm, eps)
        b, c, h, w = x.shape
        heads = temperature.shape[0]
        cpg = c // heads
        hw = h * w
        qkv = jnp.einsum('bchw,oc->bohw', x, qkv_w[:, :, 0, 0, 0])
        qkv = _conv3d(qkv[:, :, None], qkv_dw_w, groups=3 * c, pad=1)[:, :, 0]
        f_all = qkv.reshape(b, hw, 3 * heads, cpg).transpose(0, 2, 1, 3)
        f9 = jnp.einsum('bgnc,og->bonc', f_all, fc_w[:, :, 0, 0, 0]) + fc_b[None, :, None, None]
        f_conv = f9.transpose(0, 3, 1, 2).reshape(b, 9 * cpg, h, w)
        out_conv = _conv3d(f_conv[:, :, None], dep_w, groups=cpg, pad=1)[:, :, 0] + dep_b[None, :, None, None]
        q, k, v = jnp.split(qkv, 3, axis=1)
        q = _l2norm(q.reshape(b, heads, cpg, hw))
        k = _l2norm(k.reshape(b, heads, cpg, hw))
        v = v.reshape(b, heads, cpg, hw)
        g = jax.nn.relu(jnp.einsum('bchw,oc->bohw', x, gate_w1[:, :, 0, 0]) + gate_b1[None, :, None, None])
        g = jax.nn.sigmoid(jnp.einsum('bchw,oc->bohw', g, gate_w2[:, :, 0, 0]) + gate_b2[None, :, None, None])
        g = jnp.nan_to_num(g, nan=0.0)
        dynamic_k = jnp.floor(cpg * jnp.mean(g)).astype(jnp.int32)
        attn = jnp.einsum('bhcn,bhdn->bhcd', q, k) * temperature
        order = jnp.argsort(-attn, axis=-1)
        ranks = jnp.argsort(order, axis=-1)
        attn = jnp.where(ranks < dynamic_k, attn, -jnp.inf)
        attn = jax.nn.softmax(attn, axis=-1)
        out = jnp.einsum('bhcd,bhdn->bhcn', attn, v).reshape(b, c, h, w)
        out = jnp.einsum('bchw,oc->bohw', out, proj_w[:, :, 0, 0, 0])
        return out + out_conv

    def _L1_conv_ref(x, Wk, Wv, Wr, Wo, ln_g, ln_b, w_decay, u):
        import jax, jax.numpy as jnp
        import numpy as np
        LN_EPS = 1e-05
        NEG_INF = -1e+38

        def wkv_scan(w, u, k, v):
            Bdim, T, C = k.shape

            def step(carry, kv_t):
                p, q, o = carry
                kt, vt = kv_t
                no = jnp.maximum(o, u + kt)
                A = jnp.exp(o - no)
                Bw = jnp.exp(u + kt - no)
                y = (A * p + Bw * vt) / (A * q + Bw)
                no2 = jnp.maximum(w + o, kt)
                A2 = jnp.exp(w + o - no2)
                B2 = jnp.exp(kt - no2)
                return ((A2 * p + B2 * vt, A2 * q + B2, no2), y)
            init = (jnp.zeros((Bdim, C), k.dtype), jnp.zeros((Bdim, C), k.dtype), jnp.full((Bdim, C), NEG_INF, k.dtype))
            kT = jnp.moveaxis(k, 1, 0)
            vT = jnp.moveaxis(v, 1, 0)
            _, ys = jax.lax.scan(step, init, (kT, vT))
            return jnp.moveaxis(ys, 0, 1)
        B, C, H, W = x.shape
        xs = jnp.transpose(x.reshape(B, C, H * W), (0, 2, 1))
        k = jnp.einsum('btc,dc->btd', xs, Wk)
        v = jnp.einsum('btc,dc->btd', xs, Wv)
        r = jnp.einsum('btc,dc->btd', xs, Wr)
        real_w = -jnp.exp(w_decay)
        x_fwd = wkv_scan(real_w, u, k, v)
        x_bwd = jnp.flip(wkv_scan(real_w, u, jnp.flip(k, 1), jnp.flip(v, 1)), 1)
        x_bi = 0.5 * (x_fwd + x_bwd)
        h = jax.nn.sigmoid(r) * x_bi
        mu = jnp.mean(h, axis=-1, keepdims=True)
        var = jnp.var(h, axis=-1, keepdims=True)
        h = (h - mu) * jax.lax.rsqrt(var + LN_EPS) * ln_g + ln_b
        out = jnp.einsum('btc,dc->btd', h, Wo)
        return jnp.transpose(out, (0, 2, 1)).reshape(B, C, H, W)

    def _gn(v, G=32, eps=1e-5):
        B_, C_, H_, W_ = v.shape
        g = v.reshape(B_, G, C_ // G, H_, W_)
        m = jnp.mean(g, axis=(2, 3, 4), keepdims=True)
        s = jnp.var(g, axis=(2, 3, 4), keepdims=True)
        return ((g - m) / jnp.sqrt(s + eps)).reshape(v.shape)

    def _ln_c(v, eps=1e-6):
        m = jnp.mean(v, axis=1, keepdims=True)
        s = jnp.var(v, axis=1, keepdims=True)
        return (v - m) / jnp.sqrt(s + eps)

    def _ln_t(v, eps=1e-5):
        m = jnp.mean(v, axis=-1, keepdims=True)
        s = jnp.var(v, axis=-1, keepdims=True)
        return (v - m) / jnp.sqrt(s + eps)

    def _to_tokens(v):
        B_, C_, H_, W_ = v.shape
        return v.reshape(B_, C_, H_ * W_).transpose(0, 2, 1)
    def _from_tokens(t, like):
        B_, C_, H_, W_ = like.shape
        return t.transpose(0, 2, 1).reshape(B_, C_, H_, W_)

    x = x + _L0_conv_ref(_gn(x), L0_conv_temperature, L0_conv_qkv_w, L0_conv_qkv_dw_w, L0_conv_proj_w, L0_conv_fc_w, L0_conv_fc_b, L0_conv_dep_w, L0_conv_dep_b, L0_conv_gate_w1, L0_conv_gate_b1, L0_conv_gate_w2, L0_conv_gate_b2)
    x = x + _L1_conv_ref(_gn(x), L1_conv_Wk, L1_conv_Wv, L1_conv_Wr, L1_conv_Wo, L1_conv_ln_g, L1_conv_ln_b, L1_conv_w_decay, L1_conv_u)
    return x


_drawn_inputs = setup_inputs


def setup_inputs(seed=0):
    import zlib

    import numpy as np

    out = dict(_drawn_inputs(seed))
    spreads = {'L0_conv_temperature': (1.0, 0.6),
     'L1_conv_ln_g': (1.0, 0.2),
     'L1_conv_ln_b': (0.0, 0.278)}
    factors = {'L0_conv_qkv_w': 8.0,
     'L0_conv_qkv_dw_w': 8.0,
     'L0_conv_proj_w': 8.0,
     'L0_conv_fc_w': 8.0,
     'L0_conv_fc_b': 2.809,
     'L0_conv_dep_w': 2.716,
     'L1_conv_w_decay': 5.044,
     'L1_conv_u': 64.0,
     'L0_conv_dep_b': 2.679}
    for name, (base, spread) in spreads.items():
        noise = np.random.default_rng([zlib.crc32(name.encode()), seed]).standard_normal(out[name].shape)
        drawn = base * np.exp(spread * noise) if base else spread * noise
        out[name] = jnp.asarray(drawn.astype(out[name].dtype))
    for name, factor in factors.items():
        out[name] = (out[name] * factor).astype(out[name].dtype)
    return out
```

```python
import concourse.bass as bass
from concourse import mybir
from contextlib import ExitStack

F = mybir.dt.float32
ALU = mybir.AluOpType
ACT = mybir.ActivationFunctionType
AX = mybir.AxisListType

B, C, H, W = 4, 192, 128, 128
HW = H * W
HEADS, CPG = 4, 48
C3 = 3 * C
G3 = 3 * HEADS
GROUPS = 32
CG = C // GROUPS
HALF = C // 2
ROW = C3 * W
PAD_IMG = (H + 2) * ROW
GN_EPS = 1e-5
LN_EPS = 1e-5


def wait(engine, sem, value):
    if isinstance(value, int) and value <= 0:
        return
    engine.wait_ge(sem, value)


def own_wait(engine, passed):
    engine.sem_inc(passed, 1)


class Stage:

    def __init__(self, nc, name):
        self.nc, self.name, self.ctx, self.sems = nc, name, ExitStack(), []

    def __enter__(self):
        return self

    def __exit__(self, *e):
        self.ctx.close()
        self.nc.clear_and_free_semaphores(self.sems)
        self.nc.all_engine_barrier()

    def sb(self, name, shape):
        return self.ctx.enter_context(self.nc.sbuf_tensor(f"{self.name}_{name}", shape, F))

    def ps(self, name, shape):
        return self.ctx.enter_context(self.nc.psum_tensor(f"{self.name}_{name}", shape, F))

    def sem(self, name):
        self.sems.append(self.nc.alloc_semaphore(f"{self.name}_{name}"))
        return self.sems[-1]

    def block(self):
        return self.ctx.enter_context(self.nc.Block())


def group_stats(nc, x, stat0):
    LOAD, BN = 4096, 512
    PER = CG * HW
    NL = PER // LOAD
    xg = x.rearrange("b (g c) h w -> (b g) (c h w)", g=GROUPS)
    with Stage(nc, "gs") as st:
        xt = st.sb("xt", [128, 2, LOAD])
        bn = st.sb("bn", [128, PER // BN * 6])
        mv = st.sb("mv", [128, 2])
        out = st.sb("out", [128, 2])
        loaded = [st.sem(f"loaded{h}") for h in range(2)]
        reduced, aggregated, rooted, scaled, stored = map(st.sem, ("reduced", "aggregated", "rooted", "scaled", "stored"))
        block = st.block()

        @block.sync
        def _(sp):
            for n in range(2):
                sp.dma_start(xt[:, n, :], xg[:, n * LOAD:(n + 1) * LOAD]).then_inc(loaded[n], 16)
            with sp.Fori(1, NL // 2) as i:
                for h in range(2):
                    sp.wait_ge(reduced, 2 * i + h - 1)
                    sp.dma_start(xt[:, h, :], xg[:, bass.ds((2 * i + h) * LOAD, LOAD)]).then_inc(loaded[h], 16)
            sp.wait_ge(scaled, 2)
            sp.dma_start(stat0, out[:, :]).then_inc(stored, 16)
            sp.wait_ge(stored, 16)

        @block.vector
        def _(dve):
            with dve.Fori(0, NL // 2) as i:
                for h in range(2):
                    dve.wait_ge(loaded[h], 16 * i + 16)
                    for k in range(LOAD // BN):
                        last = nc.vector.bn_stats(bn[:, bass.ds((2 * i + h) * (LOAD // BN * 6) + 6 * k, 6)],
                                                  xt[:, h, k * BN:(k + 1) * BN])
                    last.then_inc(reduced, 1)
            dve.wait_ge(reduced, NL)
            nc.vector.bn_aggr(mv[:, :], bn[:, :]).then_inc(aggregated, 1)
            dve.wait_ge(aggregated, 1)
            nc.vector.tensor_scalar(out[:, 1:2], mv[:, 1:2], GN_EPS, None, ALU.add).then_inc(aggregated, 1)
            dve.wait_ge(rooted, 1)
            nc.vector.reciprocal(out[:, 0:1], mv[:, 1:2]).then_inc(scaled, 1)
            dve.wait_ge(scaled, 1)
            nc.vector.tensor_scalar(out[:, 1:2], mv[:, 0:1], out[:, 0:1], -1.0, ALU.mult, ALU.mult).then_inc(scaled, 1)

        @block.scalar
        def _(act):
            act.wait_ge(aggregated, 2)
            nc.scalar.activation(mv[:, 1:2], out[:, 1:2], ACT.Sqrt).then_inc(rooted, 1)


def by_row(ap):
    return ap.rearrange("p (r w) -> p r w", w=W)


def pointwise(nc, x, stat0, w1t, gate_b1, w2t, gate_b2, u, gate_sums):
    M, NM = 112, 6
    T, SUB = 1024, 512
    NJ = HW // T
    FIRST = M - HALF
    xv = x.rearrange("b (k p) h w -> b p k (h w)", k=2)
    with Stage(nc, "pw") as st:
        wt = st.sb("wt", [HALF, 2, NM * M])
        w2 = st.sb("w2", [HALF, 1])
        b1 = st.sb("b1", [HALF, 1])
        b2 = st.sb("b2", [1, 1])
        sc = st.sb("sc", [HALF, 2, B, 2])
        xt = st.sb("xt", [HALF, 2, 2, T])
        xh = st.sb("xh", [HALF, 2, 2, T])
        ut = st.sb("ut", [M, 2, NM, T])
        gh = st.sb("gh", [HALF, 2, SUB])
        sg = st.sb("sg", [1, 2, SUB])
        g0 = st.sb("g0", [1, 2, SUB])
        gs = st.sb("gs", [1, 2 * B * NJ])
        pt = [st.ps(f"p{m}", [M, SUB]) for m in range(NM)]
        pz = st.ps("pz", [1, SUB])
        weights, gsum_stored, passed = st.sem("weights"), st.sem("gsum_stored"), st.sem("passed")
        loaded = [st.sem(f"loaded{h}") for h in range(2)]
        stored = [st.sem(f"stored{h}") for h in range(2)]
        normed, product, by_act, by_dve = map(st.sem, ("normed", "product", "by_act", "by_dve"))
        P, A, D = NM + 1, 4, 5
        RT, RS = T // W, SUB // W

        def rows_back(lo, h, m, q):
            top = RT - 1 - q * RS
            stop = top - RS
            rows = slice(top, stop if stop >= 0 else None, -1)
            return ut[lo:M, h, m, :].rearrange("p (r w) -> p r w", w=W)[:, rows, :]
        block = st.block()

        def load(sp, j, b):
            sp.dma_start(xt[:, b % 2, :, :], xv[b, :, :, bass.ds(j * T, T)]).then_inc(loaded[b % 2], 16)

        def store(sp, j, b):
            h, n = b % 2, 4 * j + b
            sp.wait_ge(by_act, 2 * A * (n + 1) + A)
            sp.wait_ge(by_dve, 2 * D * (n + 1) + 2 * D)
            own_wait(sp, passed)
            back = (NJ - 1 - j) * T
            sp.dma_start(u[0:FIRST, b, bass.ds(back, T)], ut[HALF:M, h, 0, :]).then_inc(stored[h], 16)
            sp.dma_start(u[FIRST:C3, b, bass.ds(back, T)].rearrange("(m p) t -> p m t", p=M),
                         ut[:, h, 1:NM, :]).then_inc(stored[h], 16)

        @block.sync
        def _(sp):
            sp.dma_start(wt[:, :, :], w1t.rearrange("(k p) m -> p k m", k=2)).then_inc(weights, 16)
            sp.dma_start(w2[:, :], w2t).then_inc(weights, 16)
            sp.dma_start(b1[:, :], gate_b1.rearrange("(p a) -> p a", a=1)).then_inc(weights, 16)
            sp.dma_start(b2[:, :], gate_b2.rearrange("(p a) -> p a", a=1)).then_inc(weights, 16)
            for b in range(B):
                for k in range(2):
                    g = b * GROUPS + k * (HALF // CG)
                    src = bass.AP(stat0.tensor, 2 * g, [[2, HALF // CG], [0, CG], [1, 2]])
                    sp.dma_start(sc[:, k, b, :], src).then_inc(weights, 16)
            for h in range(2):
                sp.sem_inc(stored[h], 1)
            load(sp, 0, 0)
            load(sp, 0, 1)

            def turn(j, last):
                for b in range(B):
                    if not (last and b >= 2):
                        sp.wait_ge(normed, 4 * j + b + 1)
                        load(sp, j if b < 2 else j + 1, (b + 2) % B)
                    store(sp, j, b)
            with sp.Fori(0, NJ - 1) as j:
                turn(j, False)
            turn(NJ - 1, True)
            sp.dma_start(gate_sums, gs[:, :]).then_inc(gsum_stored, 16)
            sp.wait_ge(gsum_stored, 16)
            for h in range(2):
                sp.wait_ge(stored[h], 32 * 2 * NJ + 1)

        @block.gpsimd
        def _(pool):
            pool.wait_ge(weights, 16 * 12)
            with pool.Fori(0, NJ) as j:
                for b in range(B):
                    n = 4 * j + b
                    pool.wait_ge(loaded[b % 2], 16 * (2 * j + b // 2 + 1))
                    pool.wait_ge(product, 2 * P * n + 1)
                    own_wait(pool, passed)
                    for k in range(2):
                        last = nc.gpsimd.tensor_scalar(xh[:, b % 2, k, :], xt[:, b % 2, k, :],
                                                       sc[:, k, b, 0:1], sc[:, k, b, 1:2], ALU.mult, ALU.add)
                    last.then_inc(normed, 1)

        @block.tensor
        def _(pe):
            pe.sem_inc(product, 2 * P + 1)
            pe.wait_ge(weights, 16 * 12)
            with pe.Fori(0, NJ) as j:
                for b in range(B):
                    for q in range(2):
                        s = (4 * j + b) * 2 + q
                        if q == 0:
                            pe.wait_ge(normed, 4 * j + b + 1)
                        evacuated = [(by_act, A * s + 1), (by_dve, D * s + D + 2), (by_act, A * s + 2),
                                     (by_dve, D * s + D + 3), (by_act, A * s + 3), (by_dve, D * s + D + 4)]
                        for m in range(NM):
                            pe.wait_ge(*evacuated[m])
                            if m == 0:
                                pe.wait_ge(by_dve, D * s + D + 1)
                            for k in range(2):
                                mm = nc.tensor.matmul(pt[m][:, :], wt[:, k, m * M:(m + 1) * M],
                                                      xh[:, b % 2, k, q * SUB:(q + 1) * SUB],
                                                      start=k == 0, stop=k == 1)
                            mm.then_inc(product, 1)
                        pe.wait_ge(by_act, A * s + A + 1)
                        nc.tensor.matmul(pz[:, :], w2[:, :], gh[:, q, :], start=True, stop=True).then_inc(product, 1)

        @block.scalar
        def _(act):
            act.sem_inc(by_act, A)
            act.wait_ge(weights, 16 * 12)
            with act.Fori(0, NJ) as j:
                for b in range(B):
                    for q in range(2):
                        s = (4 * j + b) * 2 + q
                        cols = slice(q * SUB, (q + 1) * SUB)
                        act.wait_ge(product, 2 * P + P * s + 2)
                        nc.scalar.activation(gh[:, q, :], pt[0][0:HALF, :], ACT.Relu, bias=b1[:, 0:1]).then_inc(by_act, 1)
                        if q == 0:
                            act.wait_ge(stored[b % 2], 32 * (2 * j + b // 2) + 1)
                        for m in (2, 4):
                            act.wait_ge(product, 2 * P + P * s + m + 2)
                            nc.scalar.activation(rows_back(0, b % 2, m, q), by_row(pt[m][:, :]), ACT.Copy).then_inc(by_act, 1)
                        act.wait_ge(product, 2 * P + P * s + P + 1)
                        act.wait_ge(by_dve, D * s + D)
                        nc.scalar.activation(sg[:, q, :], pz[:, :], ACT.Sigmoid, bias=b2[:, 0:1]).then_inc(by_act, 1)

        @block.vector
        def _(dve):
            dve.sem_inc(by_dve, 2 * D)
            with dve.Fori(0, NJ) as j:
                for b in range(B):
                    for q in range(2):
                        s = (4 * j + b) * 2 + q
                        cols = slice(q * SUB, (q + 1) * SUB)
                        if q == 0:
                            dve.wait_ge(stored[b % 2], 32 * (2 * j + b // 2) + 1)
                        dve.wait_ge(product, 2 * P + P * s + 2)
                        nc.vector.tensor_copy(rows_back(HALF, b % 2, 0, q), by_row(pt[0][HALF:M, :])).then_inc(by_dve, 1)
                        for m in (1, 3, 5):
                            dve.wait_ge(product, 2 * P + P * s + m + 2)
                            nc.vector.tensor_copy(rows_back(0, b % 2, m, q), by_row(pt[m][:, :])).then_inc(by_dve, 1)
                        dve.wait_ge(by_act, A * s + 2 * A)
                        nc.vector.tensor_scalar(g0[:, q, :], sg[:, q, :], 0.0, None, ALU.max, ALU.add,
                                                accum_out=gs[:, bass.ds(s, 1)]).then_inc(by_dve, 1)


def depthwise(nc, u, dww, bands, d):
    GC = 8
    CQK = 2 * C
    NG = CQK // GC
    BL = 256
    CP = CQK // 96
    VC = 64
    NV = C // VC
    VR = 16
    NR = H // 2 // VR
    S = NV * NR
    NZD = 2 * B
    assert B * S == NG and NR % 2 == 0
    uv = u.rearrange("c b (h w) -> h (c b) w", w=W)
    with Stage(nc, "dw") as st:
        wsm = st.sb("wsm", [96, CP, 9])
        wv = st.sb("wv", [128, NV, 9])
        band = st.sb("band", [96, CP, 3, BL])
        zero = st.sb("zero", [128, ROW // 128])
        it = st.sb("it", [128, 2, GC * B, W + 2])
        tt = st.sb("tt", [128, 2, GC * 3, H])
        ot = st.sb("ot", [128, 2, GC, B * W])
        vi = st.sb("vi", [128, 2, VR + 2, W + 2])
        vo = st.sb("vo", [128, 2, VR, W])
        po = [st.ps(f"p{c}", [128, B * W]) for c in range(GC)]
        wl, cleared, placed, bands_stored, zeros_stored, padded = map(
            st.sem, ("wl", "cleared", "placed", "bands_stored", "zeros_stored", "padded"))
        v_weights, passed = st.sem("v_weights"), st.sem("passed")
        loaded = [st.sem(f"loaded{h}") for h in range(2)]
        stored = [st.sem(f"stored{h}") for h in range(2)]
        v_loaded = [st.sem(f"v_loaded{h}") for h in range(2)]
        v_stored = [st.sem(f"v_stored{h}") for h in range(2)]
        product, by_act, tapped = map(st.sem, ("product", "by_act", "tapped"))
        block = st.block()

        def load(sp, n, h):
            for k in range(4):
                sp.dma_start(it[:, h, k * GC:(k + 1) * GC, 1:W + 1],
                             uv[:, bass.ds(n * (GC * B) + k * GC, GC), :]).then_inc(loaded[h], 16)
            rows = bands[bass.ds(n * (GC * 3), GC * 3), :]
            src = bass.AP(rows.tensor, rows.offset, [[1, H], [BL, GC * 3], [1, H]])
            sp.dma_start(tt[:, h, :, :], src).then_inc(loaded[h], 16)

        def store(sp, n, h):
            sp.wait_ge(by_act, GC * (n + 2))
            for b in range(B):
                img = d[b, ROW:ROW + C3 * HW].rearrange("(c h w) -> h c w", h=H, w=W)
                sp.dma_start(img[:, bass.ds(n * GC, GC), :], ot[:, h, :, b * W:(b + 1) * W]).then_inc(stored[h], 16)

        def v_loads(k):
            return sum(2 + (r % NR in (0, NR - 1)) for r in k)

        def load_v(sp, b, k):
            g, r = divmod(k, NR)
            c0 = CQK + VC * g
            for half in range(2):
                lo = H // 2 * half + VR * r - 1
                first, last = max(lo, 0), min(lo + VR + 2, H)
                part = slice(VC * half, VC * half + VC)
                src = u[c0:c0 + VC, b, first * W:last * W].rearrange("c (h w) -> c h w", w=W)
                sp.dma_start(vi[part, k % 2, first - lo:last - lo, 1:W + 1], src).then_inc(v_loaded[k % 2], 16)
                if last - first < VR + 2:
                    slot = 0 if lo < 0 else VR + 1
                    sp.dma_start(vi[part, k % 2, slot, 1:W + 1],
                                 d[0, 0:VC * W].rearrange("(p w) -> p w", w=W)).then_inc(v_loaded[k % 2], 16)

        def store_v(sp, b, k):
            g, r = divmod(k, NR)
            c0 = CQK + VC * g
            for half in range(2):
                top = H - VR - H // 2 * half - VR * r
                img = image(d, b)
                sp.dma_start(img[c0:c0 + VC, top * W:(top + VR) * W],
                             vo[VC * half:VC * half + VC, k % 2].rearrange("p h w -> p (h w)")).then_inc(v_stored[k % 2], 16)

        @block.sync
        def _(sp):
            sp.dma_start(wsm[:, :, :], dww[0:CQK].rearrange("(p i) a d y x -> p (a i) (d y x)", i=CP)[:, :, 9:18]).then_inc(wl, 16)
            wvv = dww[CQK:C3].rearrange("(g p) a d y x -> p (a g) (d y x)", p=VC)[:, :, 9:18]
            for half in range(2):
                sp.dma_start(wv[VC * half:VC * half + VC, :, :], wvv).then_inc(v_weights, 16)
            sp.wait_ge(placed, 3)
            sp.dma_start(bands.rearrange("(p i x) l -> p (i x l)", p=96, x=3),
                         band[:, :, :, :].rearrange("p i x l -> p (i x l)")).then_inc(bands_stored, 16)
            sp.wait_ge(cleared, 2)
            for b in range(B):
                for at in (0, PAD_IMG - ROW):
                    sp.dma_start(d[b, at:at + ROW].rearrange("(p n) -> p n", p=128), zero[:, :]).then_inc(zeros_stored, 16)
            sp.wait_ge(zeros_stored, 16 * NZD)
            sp.wait_ge(bands_stored, 16)
            sp.wait_ge(padded, 1)
            for h in range(2):
                sp.sem_inc(stored[h], 1)
                sp.sem_inc(v_stored[h], 1)
                load_v(sp, 0, h)
                load(sp, h, h)

            def turns(b, last):
                for k in range(S):
                    n, h = S * b + k, k % 2
                    sp.wait_ge(product, GC * (n + 1))
                    if not (last and k >= S - 2):
                        load(sp, n + 2, h)
                    sp.wait_ge(tapped, 9 * (n + 1))
                    own_wait(sp, passed)
                    if not (last and k >= S - 2):
                        load_v(sp, b if k < S - 2 else b + 1, (k + 2) % S)
                    store_v(sp, b, k)
                    store(sp, n, h)
            with sp.Fori(0, B - 1) as b:
                turns(b, False)
            turns(B - 1, True)
            for h in range(2):
                sp.wait_ge(stored[h], 16 * B * (NG // 2) + 1)
                sp.wait_ge(v_stored[h], 32 * (NG // 2) + 1)

        @block.gpsimd
        def _(pool):
            for ten in (it, vi):
                nc.gpsimd.memset(ten[:, :, :, 0:1], 0.0)
                last = nc.gpsimd.memset(ten[:, :, :, W + 1:W + 2], 0.0)
            last.then_inc(padded, 1)

        @block.tensor
        def _(pe):
            with pe.Fori(0, NG // 2) as i:
                for h in range(2):
                    n = 2 * i + h
                    pe.wait_ge(loaded[h], 80 * i + 80)
                    for c in range(GC):
                        pe.wait_ge(by_act, GC * n + c + 1)
                        for dx in range(3):
                            mm = nc.tensor.matmul(po[c][:, :].rearrange("p (b w) -> p b w", b=B),
                                                  tt[:, h, 3 * c + dx, :],
                                                  it[:, h, B * c:B * (c + 1), dx:dx + W],
                                                  start=dx == 0, stop=dx == 2)
                        mm.then_inc(product, 1)

        @block.scalar
        def _(act):
            act.sem_inc(by_act, GC)
            with act.Fori(0, NG // 2) as i:
                for h in range(2):
                    n = 2 * i + h
                    act.wait_ge(stored[h], 16 * B * i + 1)
                    for c in range(GC):
                        act.wait_ge(product, GC * n + c + 1)
                        nc.scalar.activation(ot[:, h, c, :], po[c][:, :], ACT.Copy).then_inc(by_act, 1)

        @block.vector
        def _(dve):
            nc.vector.memset(band[:, :, :, :], 0.0).then_inc(cleared, 1)
            nc.vector.memset(zero[:, :], 0.0).then_inc(cleared, 1)
            dve.wait_ge(wl, 16)
            dve.wait_ge(cleared, 1)
            for dy in range(3):
                nc.vector.tensor_copy(band[:, :, :, H - dy:H - dy + 1],
                                      wsm[:, :, 3 * dy:3 * dy + 3].rearrange("p i (x a) -> p i x a", a=1)).then_inc(placed, 1)
            dve.wait_ge(v_weights, 32)
            with dve.Fori(0, B) as b:
                for k in range(S):
                    g, h, n = k // NR, k % 2, S * b + k
                    dve.wait_ge(v_loaded[h], 16 * (v_loads(range(h, S, 2)) * b + v_loads(range(h, k + 1, 2))))
                    dve.wait_ge(v_stored[h], 32 * (S // 2 * b + k // 2) + 1)
                    for tap in range(9):
                        dy, dx = divmod(tap, 3)
                        top = VR + 1 - dy
                        rows = slice(top, top - VR if top >= VR else None, -1)
                        src, w = vi[:, h, rows, dx:dx + W], wv[:, g, tap:tap + 1]
                        if tap == 0:
                            nc.vector.tensor_scalar(vo[:, h], src, w, None, ALU.mult).then_inc(tapped, 1)
                        else:
                            dve.wait_ge(tapped, 9 * n + tap)
                            nc.vector.scalar_tensor_tensor(vo[:, h], src, w, vo[:, h], ALU.mult, ALU.add).then_inc(tapped, 1)


def image(d, b):
    return d[b, ROW:ROW + C3 * HW].rearrange("(c t) -> c t", t=HW)


def gram(nc, d, gram_d):
    QK = 2 * CPG
    with Stage(nc, "gr") as st:
        qk = st.sb("qk", [128, 2, QK, W])
        g = st.sb("g", [QK, B * HEADS, QK])
        pg = [st.ps(f"p{h}", [QK, QK]) for h in range(2)]
        loaded = [st.sem(f"loaded{h}") for h in range(2)]
        product, copied, stored = map(st.sem, ("product", "copied", "stored"))
        block = st.block()

        @block.sync
        def _(sp):
            with sp.Fori(0, B) as b:
                for hd in range(HEADS):
                    sp.wait_ge(product, HEADS * b + hd + 1)
                    for k in range(2):
                        img = image(d, b).rearrange("c (h w) -> h c w", h=H)
                        c0 = k * C + hd * CPG
                        for e in range(0, CPG, 12):
                            sp.dma_start(qk[:, hd % 2, k * CPG + e:k * CPG + e + 12, :],
                                         img[:, c0 + e:c0 + e + 12, :]).then_inc(loaded[hd % 2], 16)
            sp.wait_ge(copied, B * HEADS + 2)
            sp.dma_start(gram_d, g[:, :, :]).then_inc(stored, 16)
            sp.wait_ge(stored, 16)

        @block.tensor
        def _(pe):
            pe.sem_inc(product, 2)
            with pe.Fori(0, B) as b:
                for hd in range(HEADS):
                    pe.wait_ge(loaded[hd % 2], 256 * b + 128 * (hd // 2 + 1))
                    pe.wait_ge(copied, HEADS * b + hd + 1)
                    for w in range(W):
                        tok = qk[:, hd % 2, :, w]
                        mm = nc.tensor.matmul(pg[hd % 2][:, :], tok, tok, start=w == 0, stop=w == W - 1)
                    mm.then_inc(product, 1)

        @block.vector
        def _(dve):
            dve.sem_inc(copied, 2)
            with dve.Fori(0, B) as b:
                for hd in range(HEADS):
                    dve.wait_ge(product, HEADS * b + hd + 3)
                    nc.vector.tensor_copy(g[:, bass.ds(HEADS * b + hd, 1), :].rearrange("p a c -> p (a c)"),
                                          pg[hd % 2][:, :]).then_inc(copied, 1)


def attention_scores(nc, gram_d, temperature, attn_d):
    QK, NI = 2 * CPG, B * HEADS
    with Stage(nc, "as") as st:
        g = st.sb("g", [QK, NI, QK])
        gd = st.sb("gd", [QK, NI, QK])
        ident = st.sb("ident", [QK, QK])
        ones = st.sb("ones", [QK, QK])
        nrm = st.sb("nrm", [QK, NI, QK])
        nq = st.sb("nq", [CPG, NI])
        temp = st.sb("temp", [CPG, HEADS])
        a = st.sb("a", [CPG, NI, CPG])
        pd = st.ps("pd", [QK, 3, 512])
        loaded, consts, step, diag, rooted, stored = map(st.sem, ("loaded", "consts", "step", "diag", "rooted", "stored"))
        block = st.block()

        @block.sync
        def _(sp):
            sp.dma_start(g[:, :, :], gram_d).then_inc(loaded, 16)
            sp.dma_start(temp[:, :], bass.AP(temperature.tensor, 0, [[0, CPG], [1, HEADS]])).then_inc(loaded, 16)
            sp.wait_ge(step, 9)
            sp.dma_start(attn_d, a[:, :, :]).then_inc(stored, 16)
            sp.wait_ge(stored, 16)

        @block.gpsimd
        def _(pool):
            nc.gpsimd.memset(ones[:, :], 1.0).then_inc(consts, 1)
            nc.gpsimd.memset(ident[:, :], 0.0).then_inc(consts, 1)
            pool.wait_ge(consts, 2)
            nc.gpsimd.affine_select(out=ident[:, :], in_=ident[:, :], compare_op=ALU.not_equal, fill=1.0,
                                    base=0, pattern=[[-1, QK]], channel_multiplier=1).then_inc(consts, 1)

        @block.vector
        def _(dve):
            dve.wait_ge(loaded, 32)
            dve.wait_ge(consts, 3)
            idb = ident[:, :].rearrange("p (a k) -> p a k", a=1).to_broadcast([QK, NI, QK])
            nc.vector.tensor_tensor(gd[:, :, :], g[:, :, :], idb, ALU.mult).then_inc(step, 1)
            dve.wait_ge(step, 1)
            nc.vector.tensor_reduce(nq[:, :], gd[0:CPG, :, :], AX.X, ALU.add).then_inc(step, 1)
            dve.wait_ge(rooted, 2)
            nc.vector.tensor_scalar(nrm[:, :, :], nrm[:, :, :], 1e-12, None, ALU.max).then_inc(step, 1)
            nc.vector.tensor_scalar(nq[:, :], nq[:, :], 1e-12, None, ALU.max).then_inc(step, 1)
            dve.wait_ge(step, 4)
            nc.vector.reciprocal(nrm[0:CPG, :, CPG:QK], nrm[0:CPG, :, CPG:QK]).then_inc(step, 1)
            nc.vector.reciprocal(nq[:, :], nq[:, :]).then_inc(step, 1)
            dve.wait_ge(step, 6)
            nc.vector.tensor_tensor(a[:, :, :], g[0:CPG, :, CPG:QK], nrm[0:CPG, :, CPG:QK], ALU.mult).then_inc(step, 1)
            dve.wait_ge(step, 7)
            nqb = nq[:, :].rearrange("p (n a) -> p n a", a=1).to_broadcast([CPG, NI, CPG])
            nc.vector.tensor_tensor(a[:, :, :], a[:, :, :], nqb, ALU.mult).then_inc(step, 1)
            dve.wait_ge(step, 8)
            for hd in range(HEADS):
                av = a[:, :, :].rearrange("p (b h) k -> p b h k", h=HEADS)[:, :, hd, :]
                last = nc.vector.tensor_scalar(av, av, temp[:, hd:hd + 1], None, ALU.mult)
            last.then_inc(step, 1)

        @block.tensor
        def _(pe):
            pe.wait_ge(step, 1)
            gf = gd[:, :, :].rearrange("p n k -> p (n k)")
            for t in range(3):
                last = nc.tensor.matmul(pd[:, t, :], ones[:, :], gf[:, t * 512:(t + 1) * 512], start=True, stop=True)
            last.then_inc(diag, 1)

        @block.scalar
        def _(act):
            act.wait_ge(diag, 1)
            nc.scalar.activation(nrm[:, :, :].rearrange("p n k -> p (n k)"), pd[:, :, :].rearrange("p a b -> p (a b)"),
                                 ACT.Sqrt).then_inc(rooted, 1)
            act.wait_ge(step, 2)
            nc.scalar.activation(nq[:, :], nq[:, :], ACT.Sqrt).then_inc(rooted, 1)


def branch_conv(nc, x, d, fcb, branch_w, branch_b, flags, attn_d, rank_d, t):
    RIN, ROUT = 10, 8
    KZ = RIN * G3
    K = KZ + 3
    NB = H // ROUT
    NI = B * HEADS
    JJ = C // CPG
    CQ = CPG // 4
    zv = d.rearrange("b (r w g c) -> b r g w c", w=W, g=G3, c=CPG)
    with Stage(nc, "bc") as st:
        taps = st.sb("taps", [10, C, 9])
        fcr = st.sb("fcr", [10, G3 + 1])
        fcx = st.sb("fcx", [10, K])
        mask = st.sb("mask", [K, 3, ROUT])
        wc = st.sb("wc", [K, CPG, 3, JJ, ROUT])
        tmp = st.sb("tmp", [K, CPG, JJ, ROUT])
        z = st.sb("z", [K, 2, 2, W + 2, CPG])
        flag = z[0:3 * NB, 0, 0, :, :]
        xt = st.sb("xt", [128, 2, CQ, 2, W])
        a = st.sb("a", [CPG, NI, CPG])
        tri = st.sb("tri", [CPG, CPG, CPG])
        gt = st.sb("gt", [CPG, CPG, CPG])
        eq = st.sb("eq", [CPG, CPG, CPG])
        rank = st.sb("rank", [CPG, NI, CPG])
        pr = [st.ps(f"r{k}", [K, C]) for k in range(2)]
        NBANK = 6
        po = [st.ps(f"p{k}", [128, 2, W]) for k in range(NBANK)]
        wl, consts, spread, rprod, rmade, flags_stored, al, ranked, rank_stored = map(
            st.sem, ("wl", "consts", "spread", "rprod", "rmade", "flags_stored", "al", "ranked", "rank_stored"))
        z_loaded = [st.sem(f"z_loaded{h}") for h in range(2)]
        x_loaded = [st.sem(f"x_loaded{h}") for h in range(2)]
        stored = [st.sem(f"stored{h}") for h in range(2)]
        product, added, cmp = map(st.sem, ("product", "added", "cmp"))
        block = st.block()
        NZ = 2 * RIN + 2

        def load(sp, i, h):
            for bb in range(2):
                b = 2 * h + bb
                for r in range(RIN):
                    sp.dma_start(z[r * G3:(r + 1) * G3, h, bb, 1:W + 1, :],
                                 zv[b, bass.ds(ROUT * i + r, 1)].rearrange("a g w c -> (a g) w c")).then_inc(z_loaded[h], 16)
                sp.dma_start(z[KZ:K, h, bb, :, :], flags[bass.ds(3 * i, 3)]).then_inc(z_loaded[h], 16)

        def load_x(sp, i, h):
            for bb in range(2):
                for q in range(CQ):
                    sp.dma_start(xt[:, h, q, bb, :], rows16(x, 2 * h + bb, q, i)).then_inc(x_loaded[h], 16)

        def rows16(ten, b, q, i):
            return ten[b, 16 * q:16 * q + 16, bass.ds(ROUT * i, ROUT), :]

        def store(act, i, h):
            act.wait_ge(added, NBANK + 2 * CQ * i + CQ * (h + 1))
            for bb in range(2):
                for q in range(CQ):
                    act.dma_start(rows16(t, 2 * h + bb, q, i), xt[:, h, q, bb, :]).then_inc(stored[h], 16)

        @block.sync
        def _(sp):
            sp.wait_ge(consts, 2)
            dv = branch_w.rearrange("c o d y x -> o c (d y x)")
            sp.dma_start(taps[0:9, :, :], dv[:, :, 9:18]).then_inc(wl, 16)
            sp.dma_start(taps[9:10, :, 4:5], branch_b.rearrange("(a c k) -> a c k", a=1, k=1),
                         allow_slow_non_contiguous=True).then_inc(wl, 16)
            sp.dma_start(fcr[0:9, :], fcb).then_inc(wl, 16)
            sp.dma_start(a[:, :, :], attn_d).then_inc(al, 16)
            sp.wait_ge(consts, 6)
            sp.dma_start(flags, flag).then_inc(flags_stored, 16)
            sp.wait_ge(flags_stored, 16)
            for h in range(2):
                load(sp, 0, h)
            with sp.Fori(0, NB - 1) as i:
                for h in range(2):
                    sp.wait_ge(product, 2 * CQ * i + CQ * (h + 1))
                    load(sp, i + 1, h)
            sp.wait_ge(ranked, NI)
            sp.dma_start(rank_d, rank[:, :, :]).then_inc(rank_stored, 16)
            sp.wait_ge(rank_stored, 16)
            for h in range(2):
                sp.wait_ge(stored[h], 16 * 2 * CQ * NB)

        @block.gpsimd
        def _(pool):
            nc.gpsimd.memset(taps[:, :, :], 0.0).then_inc(consts, 1)
            nc.gpsimd.memset(fcr[:, 0:G3], 0.0)
            nc.gpsimd.memset(fcr[:, G3:G3 + 1], 1.0).then_inc(consts, 1)
            nc.gpsimd.memset(mask[:, :, :], 1.0)
            nc.gpsimd.memset(z[:, :, :, 0:1, :], 0.0)
            nc.gpsimd.memset(z[:, :, :, W + 1:W + 2, :], 0.0)
            nc.gpsimd.memset(tri[:, :, :], 1.0)
            nc.gpsimd.memset(flag[:, 1:W + 1, :], 1.0).then_inc(consts, 1)
            pool.wait_ge(consts, 3)
            inner = flag[:, 1:W + 1, :]
            nc.gpsimd.affine_select(out=inner, in_=inner, compare_op=ALU.not_equal, fill=0.0, base=-1,
                                    pattern=[[0, W], [0, CPG]], channel_multiplier=1).then_inc(consts, 1)
            pool.wait_ge(consts, 4)
            nc.gpsimd.affine_select(out=inner, in_=inner, compare_op=ALU.not_equal, fill=0.0, base=-(3 * NB - 1),
                                    pattern=[[0, W], [0, CPG]], channel_multiplier=1).then_inc(consts, 1)
            nc.gpsimd.affine_select(out=tri[:, :, :], in_=tri[:, :, :], compare_op=ALU.is_gt, fill=0.0, base=0,
                                    pattern=[[1, CPG], [-1, CPG]], channel_multiplier=0).then_inc(consts, 1)
            pool.wait_ge(consts, 6)
            pat = [[-G3, 3], [-G3, ROUT]]
            nc.gpsimd.affine_select(out=mask[:, :, :], in_=mask[:, :, :], compare_op=ALU.is_ge, fill=0.0, base=0,
                                    pattern=pat, channel_multiplier=1).then_inc(consts, 1)
            pool.wait_ge(consts, 7)
            nc.gpsimd.affine_select(out=mask[:, :, :], in_=mask[:, :, :], compare_op=ALU.is_ge, fill=0.0, base=G3 - 1,
                                    pattern=[[G3, 3], [G3, ROUT]], channel_multiplier=-1).then_inc(consts, 1)
            pool.wait_ge(consts, 8)
            nc.gpsimd.affine_select(out=mask[:, :, :], in_=mask[:, :, :], compare_op=ALU.not_equal, fill=1.0, base=-KZ,
                                    pattern=[[0, 3], [0, ROUT]], channel_multiplier=1).then_inc(consts, 1)
            pool.wait_ge(consts, 9)
            for n, (row, dy, rout, fill) in enumerate(((0, 0, 0, 0.0), (0, 2, ROUT - 1, 0.0), (1, 0, 0, 1.0), (2, 2, ROUT - 1, 1.0))):
                nc.gpsimd.affine_select(out=mask[:, :, :], in_=mask[:, :, :], compare_op=ALU.not_equal, fill=fill,
                                        base=-(KZ + row) - 1000 * dy - 10000 * rout,
                                        pattern=[[1000, 3], [10000, ROUT]], channel_multiplier=1).then_inc(consts, 1)
                pool.wait_ge(consts, 10 + n)

        @block.scalar
        def _(act):
            for h in range(2):
                load_x(act, 0, h)
            with act.Fori(0, NB - 1) as i:
                for h in range(2):
                    store(act, i, h)
                    act.wait_ge(stored[h], 16 * 2 * CQ * (i + 1))
                    load_x(act, i + 1, h)
            for h in range(2):
                store(act, NB - 1, h)

        @block.tensor
        def _(pe):
            pe.wait_ge(spread, 2)
            pe.wait_ge(wl, 48)
            for n in range(9):
                wait(pe, rmade, 2 * (n - 1))
                nc.tensor.matmul(pr[n % 2][:, :], fcx[:, :], taps[:, :, n], start=True, stop=True).then_inc(rprod, 1)
            pe.wait_ge(rmade, 19)
            with pe.Fori(0, NB) as i:
                for h in range(2):
                    pe.wait_ge(z_loaded[h], 16 * NZ * (i + 1))
                    for q in range(CQ):
                        pe.wait_ge(added, 2 * CQ * i + CQ * h + q + 1)
                        for dx in range(3):
                            for c4 in range(4):
                                c = 4 * q + c4
                                mm = nc.tensor.matmul(po[q % NBANK][32 * c4:32 * c4 + 32, :, :],
                                                      wc[:, c, dx, :, :].rearrange("p j r -> p (j r)"),
                                                      z[:, h, :, dx:dx + W, c], start=dx == 0, stop=dx == 2,
                                                      skip_group_check=True)
                        mm.then_inc(product, 1)

        @block.vector
        def _(dve):
            dve.wait_ge(wl, 48)
            nc.vector.tensor_copy(fcx[:, 0:KZ].rearrange("p (r g) -> p r g", g=G3),
                                  fcr[:, 0:G3].rearrange("p (a g) -> p a g", a=1).to_broadcast([10, RIN, G3])).then_inc(spread, 1)
            nc.vector.tensor_copy(fcx[:, KZ:K], fcr[:, G3:G3 + 1].to_broadcast([10, 3])).then_inc(spread, 1)
            dve.wait_ge(consts, 13)
            nc.vector.memset(wc[:, :, :, :, :], 0.0).then_inc(rmade, 1)
            for n in range(9):
                dy, dx = divmod(n, 3)
                dve.wait_ge(rprod, n + 1)
                dve.wait_ge(rmade, 2 * n + 1)
                src = pr[n % 2][:, :].rearrange("p (c j a) -> p c j a", j=JJ, a=1).to_broadcast([K, CPG, JJ, ROUT])
                m = mask[:, dy, :].rearrange("p (a b r) -> p a b r", a=1, b=1).to_broadcast([K, CPG, JJ, ROUT])
                nc.vector.tensor_tensor(tmp[:, :, :, :], src, m, ALU.mult).then_inc(rmade, 1)
                dve.wait_ge(rmade, 2 * n + 2)
                nc.vector.tensor_tensor(wc[:, :, dx, :, :], wc[:, :, dx, :, :], tmp[:, :, :, :], ALU.add).then_inc(rmade, 1)
            dve.wait_ge(al, 16)
            dve.sem_inc(added, NBANK)
            dve.wait_ge(rmade, 19)
            with dve.Fori(0, NB) as i:
                for h in range(2):
                    dve.wait_ge(x_loaded[h], 16 * 2 * CQ * (i + 1))
                    for q in range(CQ):
                        dve.wait_ge(product, 2 * CQ * i + CQ * h + q + 1)
                        nc.vector.tensor_tensor(xt[:, h, q, :, :], po[q % NBANK][:, :, :], xt[:, h, q, :, :],
                                                ALU.add).then_inc(added, 1)
                ai = a[:, bass.ds(i, 1), :].to_broadcast([CPG, CPG, CPG])
                aj = a[:, bass.ds(i, 1), :].rearrange("p a j -> p j a").to_broadcast([CPG, CPG, CPG])
                nc.vector.tensor_tensor(gt[:, :, :], ai, aj, ALU.is_gt).then_inc(cmp, 1)
                nc.vector.tensor_tensor(eq[:, :, :], ai, aj, ALU.is_equal).then_inc(cmp, 1)
                dve.wait_ge(cmp, 4 * i + 2)
                nc.vector.tensor_tensor(eq[:, :, :], eq[:, :, :], tri[:, :, :], ALU.mult).then_inc(cmp, 1)
                dve.wait_ge(cmp, 4 * i + 3)
                nc.vector.tensor_tensor(gt[:, :, :], gt[:, :, :], eq[:, :, :], ALU.add).then_inc(cmp, 1)
                dve.wait_ge(cmp, 4 * i + 4)
                nc.vector.tensor_reduce(rank[:, bass.ds(i, 1), :].rearrange("p a j -> p (a j)"), gt[:, :, :],
                                        AX.X, ALU.add).then_inc(ranked, 1)


def attention_weights(nc, attn_d, rank_d, gate_sums, projt, pt_d):
    NI = B * HEADS
    NS = gate_sums.shape[1]
    with Stage(nc, "aw") as st:
        a = st.sb("a", [CPG, NI, CPG])
        e = st.sb("e", [CPG, NI, CPG])
        rank = st.sb("rank", [CPG, NI, CPG])
        mx = st.sb("mx", [CPG, NI])
        sm = st.sb("sm", [CPG, NI])
        gsum = st.sb("gsum", [1, NS])
        g1 = st.sb("g1", [1, 1])
        ones = st.sb("ones", [1, CPG])
        kk = st.sb("kk", [CPG, 1])
        pj = st.sb("pj", [CPG, HEADS, C])
        ptt = st.sb("ptt", [CPG, NI, C])
        pk = st.ps("pk", [CPG, 1])
        po = [st.ps(f"p{k}", [CPG, C]) for k in range(2)]
        loaded, step, kb, product, copied, expd, stored = map(
            st.sem, ("loaded", "step", "kb", "product", "copied", "expd", "stored"))
        block = st.block()

        @block.sync
        def _(sp):
            sp.dma_start(a[:, :, :], attn_d).then_inc(loaded, 16)
            sp.dma_start(rank[:, :, :], rank_d).then_inc(loaded, 16)
            sp.dma_start(gsum[:, :], gate_sums).then_inc(loaded, 16)
            sp.dma_start(pj[:, :, :], projt.rearrange("(h c) o -> c h o", h=HEADS)).then_inc(loaded, 16)
            for b in range(B):
                sp.wait_ge(copied, HEADS * (b + 1))
                sp.dma_start(pt_d[b].rearrange("(h c) o -> c h o", h=HEADS), ptt[:, HEADS * b:HEADS * (b + 1), :]).then_inc(stored, 16)
            sp.wait_ge(stored, 16 * B)

        @block.vector
        def _(dve):
            nc.vector.memset(ones[:, :], 1.0)
            dve.wait_ge(loaded, 64)
            nc.vector.tensor_reduce(g1[:, :], gsum[:, :], AX.X, ALU.add).then_inc(step, 1)
            nc.vector.tensor_reduce(mx[:, :], a[:, :, :], AX.X, ALU.max).then_inc(step, 1)
            dve.wait_ge(step, 2)
            nc.vector.tensor_tensor(a[:, :, :], a[:, :, :], mx[:, :].rearrange("p (n a) -> p n a", a=1).to_broadcast([CPG, NI, CPG]),
                                    ALU.subtract).then_inc(step, 1)
            dve.wait_ge(kb, 1)
            nc.vector.tensor_scalar(kk[:, :], pk[:, :], float(CPG) / (B * HW), -1.0, ALU.mult, ALU.add).then_inc(step, 1)
            dve.wait_ge(step, 4)
            nc.vector.tensor_scalar(rank[:, :, :], rank[:, :, :], kk[:, 0:1], None, ALU.is_le).then_inc(step, 1)
            dve.wait_ge(step, 5)
            dve.wait_ge(expd, 1)
            nc.vector.tensor_tensor(e[:, :, :], e[:, :, :], rank[:, :, :], ALU.mult).then_inc(step, 1)
            dve.wait_ge(step, 6)
            nc.vector.tensor_reduce(sm[:, :], e[:, :, :], AX.X, ALU.add).then_inc(step, 1)
            dve.wait_ge(step, 7)
            nc.vector.reciprocal(sm[:, :], sm[:, :]).then_inc(step, 1)
            dve.wait_ge(step, 8)
            nc.vector.tensor_tensor(e[:, :, :], e[:, :, :], sm[:, :].rearrange("p (n a) -> p n a", a=1).to_broadcast([CPG, NI, CPG]),
                                    ALU.mult).then_inc(step, 1)
            for n in range(NI):
                dve.wait_ge(product, n + 1)
                nc.vector.tensor_copy(ptt[:, n, :], po[n % 2][:, :]).then_inc(copied, 1)

        @block.scalar
        def _(act):
            act.wait_ge(step, 3)
            nc.scalar.activation(e[:, :, :].rearrange("p n k -> p (n k)"), a[:, :, :].rearrange("p n k -> p (n k)"),
                                 ACT.Exp).then_inc(expd, 1)

        @block.tensor
        def _(pe):
            pe.wait_ge(step, 1)
            nc.tensor.matmul(pk[:, :], ones[:, :], g1[:, :], start=True, stop=True).then_inc(kb, 1)
            pe.wait_ge(step, 9)
            for n in range(NI):
                wait(pe, copied, n - 1)
                nc.tensor.matmul(po[n % 2][:, :], e[:, n, :], pj[:, n % HEADS, :], start=True, stop=True).then_inc(product, 1)


def apply_attention(nc, d, t, pt_d, x1, stat1):
    T, SUB = 1024, 512
    NJ = HW // T
    NS = HW // SUB
    with Stage(nc, "ap") as st:
        pw = st.sb("pw", [HALF, B, 2, C])
        vt = st.sb("vt", [HALF, 2, 2, T])
        tt = st.sb("tt", [HALF, 2, 2, T])
        xo = st.sb("xo", [HALF, 2, 2, T])
        bn = st.sb("bn", [HALF, B * 2, NS * 6])
        mv = st.sb("mv", [HALF, B * 2, 2])
        sq = st.sb("sq", [HALF, B * 2, 2])
        grp = st.sb("grp", [HALF, HALF // CG, CG])
        ss = st.sb("ss", [HALF, B * 2, 2])
        po = [st.ps(f"p{k}", [HALF, SUB]) for k in range(4)]
        pgm = st.ps("pgm", [HALF, B * 4])
        weights, passed = st.sem("weights"), st.sem("passed")
        loaded = [st.sem(f"loaded{h}") for h in range(2)]
        stored = [st.sem(f"stored{h}") for h in range(2)]
        product, added, consts, step, avg, rooted, s_stored, counted = map(
            st.sem, ("product", "added", "consts", "step", "avg", "rooted", "s_stored", "counted"))
        block = st.block()
        tv = t.rearrange("b (m p) h w -> b p m (h w)", m=2)
        x1v = x1.rearrange("b (m p) t -> b p m t", m=2)

        def load(sp, j, b):
            v = image(d, b)[2 * C:3 * C, bass.ds(j * T, T)].rearrange("(k p) t -> p k t", k=2)
            sp.dma_start(vt[:, b % 2, :, :], v).then_inc(loaded[b % 2], 16)
            sp.dma_start(tt[:, b % 2, :, :], tv[b, :, :, bass.ds(j * T, T)]).then_inc(loaded[b % 2], 16)

        @block.sync
        def _(sp):
            for b in range(B):
                sp.dma_start(pw[:, b, :, :], pt_d[b].rearrange("(k p) o -> p k o", k=2)).then_inc(weights, 16)
            for h in range(2):
                sp.sem_inc(stored[h], 1)
            load(sp, 0, 0)
            load(sp, 0, 1)

            def turn(j, last):
                for b in range(B):
                    if not (last and b >= 2):
                        sp.wait_ge(added, 4 * (4 * j + b + 2))
                        own_wait(sp, passed)
                        load(sp, j if b < 2 else j + 1, (b + 2) % B)
                    sp.wait_ge(added, 4 * (4 * j + b + 2))
                    own_wait(sp, passed)
                    sp.dma_start(x1v[b, :, :, bass.ds(j * T, T)], xo[:, b % 2, :, :]).then_inc(stored[b % 2], 16)
            with sp.Fori(0, NJ - 1) as j:
                turn(j, False)
            turn(NJ - 1, True)
            sp.wait_ge(step, 5)
            for b in range(B):
                sp.dma_start(stat1[b].rearrange("(m p) s -> p m s", m=2), ss[:, 2 * b:2 * b + 2, :]).then_inc(s_stored, 16)
            sp.wait_ge(s_stored, 16 * B)
            for h in range(2):
                sp.wait_ge(stored[h], 16 * 2 * NJ + 1)

        @block.tensor
        def _(pe):
            pe.wait_ge(weights, 16 * B)
            with pe.Fori(0, NJ) as j:
                for b in range(B):
                    n = 4 * j + b
                    pe.wait_ge(loaded[b % 2], 32 * (2 * j + b // 2 + 1))
                    for q in range(2):
                        for m in range(2):
                            pe.wait_ge(added, 4 * n + 2 * q + m + 1)
                            for k in range(2):
                                mm = nc.tensor.matmul(po[2 * q + m][:, :], pw[:, b, k, m * HALF:(m + 1) * HALF],
                                                      vt[:, b % 2, k, q * SUB:(q + 1) * SUB], start=k == 0, stop=k == 1)
                            mm.then_inc(product, 1)
            pe.wait_ge(consts, 4)
            pe.wait_ge(step, 3)
            nc.tensor.matmul(pgm[:, :], grp[:, :, :].rearrange("p a b -> p (a b)"),
                             sq[:, :, :].rearrange("p a b -> p (a b)"), start=True, stop=True).then_inc(avg, 1)

        @block.gpsimd
        def _(pool):
            nc.gpsimd.memset(grp[:, :, :], 1.0 / CG).then_inc(consts, 1)
            pool.wait_ge(consts, 1)
            nc.gpsimd.affine_select(out=grp[:, :, :], in_=grp[:, :, :], compare_op=ALU.is_ge, fill=0.0, base=0,
                                    pattern=[[-CG, HALF // CG], [0, CG]], channel_multiplier=1).then_inc(consts, 1)
            pool.wait_ge(consts, 2)
            nc.gpsimd.affine_select(out=grp[:, :, :], in_=grp[:, :, :], compare_op=ALU.is_ge, fill=0.0, base=CG - 1,
                                    pattern=[[CG, HALF // CG], [0, CG]], channel_multiplier=-1).then_inc(consts, 2)

        @block.vector
        def _(dve):
            dve.sem_inc(added, 4)
            with dve.Fori(0, NJ) as j:
                for b in range(B):
                    n = 4 * j + b
                    dve.wait_ge(loaded[b % 2], 32 * (2 * j + b // 2 + 1))
                    dve.wait_ge(stored[b % 2], 16 * (2 * j + b // 2) + 1)
                    for q in range(2):
                        for m in range(2):
                            cols = slice(q * SUB, (q + 1) * SUB)
                            dve.wait_ge(product, 4 * n + 2 * q + m + 1)
                            nc.vector.tensor_tensor(xo[:, b % 2, m, cols], po[2 * q + m][:, :], tt[:, b % 2, m, cols],
                                                    ALU.add).then_inc(added, 1)
                    dve.wait_ge(added, 4 * (n + 2))
                    for q in range(2):
                        for m in range(2):
                            last = nc.vector.bn_stats(bn[:, 2 * b + m, bass.ds(12 * j + 6 * q, 6)],
                                                      xo[:, b % 2, m, q * SUB:(q + 1) * SUB])
                    last.then_inc(counted, 1)
            dve.wait_ge(counted, B * NJ)
            for n in range(2 * B):
                last = nc.vector.bn_aggr(mv[:, n, :], bn[:, n, :])
            last.then_inc(step, 1)
            dve.wait_ge(step, 1)
            nc.vector.tensor_tensor(sq[:, :, 1], mv[:, :, 0], mv[:, :, 0], ALU.mult)
            nc.vector.tensor_copy(sq[:, :, 0], mv[:, :, 0]).then_inc(step, 1)
            dve.wait_ge(step, 2)
            nc.vector.tensor_tensor(sq[:, :, 1], sq[:, :, 1], mv[:, :, 1], ALU.add).then_inc(step, 1)
            dve.wait_ge(avg, 1)
            pg = pgm[:, :].rearrange("p (n s) -> p n s", s=2)
            nc.vector.tensor_copy(mv[:, :, :], pg).then_inc(avg, 1)
            dve.wait_ge(avg, 2)
            nc.vector.tensor_tensor(sq[:, :, 0], mv[:, :, 0], mv[:, :, 0], ALU.mult).then_inc(avg, 1)
            dve.wait_ge(avg, 3)
            nc.vector.scalar_tensor_tensor(sq[:, :, 1], mv[:, :, 1], GN_EPS, sq[:, :, 0], ALU.add, ALU.subtract).then_inc(avg, 1)
            dve.wait_ge(rooted, 1)
            nc.vector.reciprocal(ss[:, :, 0], sq[:, :, 0]).then_inc(step, 1)
            dve.wait_ge(step, 4)
            nc.vector.scalar_tensor_tensor(ss[:, :, 1], mv[:, :, 0], -1.0, ss[:, :, 0], ALU.mult, ALU.mult).then_inc(step, 1)

        @block.scalar
        def _(act):
            act.wait_ge(avg, 4)
            nc.scalar.activation(sq[:, :, 0], sq[:, :, 1], ACT.Sqrt).then_inc(rooted, 1)


CH = 512
NCH = HW // CH
LO = 128
TILES = ((0, 0, 0), (1, 2, 1))


def tile_loads(sp, dst, x1, pair, tok, sem):
    b0, b1 = 2 * pair, 2 * pair + 1
    sp.dma_start(dst[:, 0, :], x1[b0, 0:LO, tok]).then_inc(sem, 16)
    sp.dma_start(dst[:, 2, :], x1[b1, 0:LO, tok]).then_inc(sem, 16)
    sp.dma_start(dst[0:64, 1, :], x1[b0, LO:C, tok]).then_inc(sem, 16)
    sp.dma_start(dst[64:128, 1, :], x1[b1, LO:C, tok]).then_inc(sem, 16)


def tile_column(sp, dst, src, sem, second=None):
    second = src if second is None else second
    sp.dma_start(dst[:, 0, :], src[0:LO]).then_inc(sem, 16)
    sp.dma_start(dst[:, 2, :], second[0:LO]).then_inc(sem, 16)
    sp.dma_start(dst[0:64, 1, :], src[LO:C]).then_inc(sem, 16)
    sp.dma_start(dst[64:128, 1, :], second[LO:C]).then_inc(sem, 16)


WA1, WA2, WC2, WB1, WB2, WN = 0, 128, 256, 384, 448, 576


def load_weight(sp, w, wt, sem):
    sp.dma_start(w[:, WA1:WA1 + LO], wt[0:LO, 0:LO]).then_inc(sem, 16)
    sp.dma_start(w[0:64, WA2:WA2 + LO], wt[LO:C, 0:LO]).then_inc(sem, 16)
    sp.dma_start(w[64:128, WC2:WC2 + LO], wt[LO:C, 0:LO]).then_inc(sem, 16)
    sp.dma_start(w[:, WB1:WB1 + 64], wt[0:LO, LO:C]).then_inc(sem, 16)
    sp.dma_start(w[0:64, WB2:WB2 + 64], wt[LO:C, LO:C]).then_inc(sem, 16)
    sp.dma_start(w[64:128, WB2 + 64:WN], wt[LO:C, LO:C]).then_inc(sem, 16)


LOADS_W = 6


def project(nc, out, w, src):
    mm = nc.tensor.matmul
    for tile, part in ((0, WA2), (2, WC2)):
        mm(out[:, tile, :], w[:, WA1:WA1 + LO], src[:, tile, :], start=True, stop=False)
        mm(out[:, tile, :], w[:, part:part + LO], src[:, 1, :], start=False, stop=True)
    mm(out[:, 1, :], w[:, WB2:WN], src[:, 1, :], start=True, stop=False, skip_group_check=True)
    mm(out[0:64, 1, :], w[:, WB1:WB1 + 64], src[:, 0, :], start=False, stop=True, skip_group_check=True)
    return mm(out[64:128, 1, :], w[:, WB1:WB1 + 64], src[:, 2, :], start=False, stop=True, skip_group_check=True)


def flat(ap):
    return ap.rearrange("p a t -> p (a t)")


def wkv_backward(nc, pair, x1, stat1, wkt, wvt, decay, bonus, k_d, v_d, y_d, mx_d):
    with Stage(nc, f"wb{pair}") as st:
        wk = st.sb("wk", [128, WN])
        wv = st.sb("wv", [128, WN])
        sc = st.sb("sc", [128, 3, 2])
        dec = st.sb("dec", [128, 3, 1])
        ew = st.sb("ew", [128, 3, 1])
        eu = st.sb("eu", [128, 3, 1])
        xt = st.sb("xt", [128, 2, 3, CH])
        xh = st.sb("xh", [128, 2, 3, CH])
        ks = st.sb("ks", [128, 2, 3, CH])
        vs = st.sb("vs", [128, 2, 3, CH])
        bt = st.sb("bt", [128, 2, 3, CH])
        bv = st.sb("bv", [128, 2, 3, CH])
        qq = st.sb("qq", [128, 2, 3, CH + 1])
        pp = st.sb("pp", [128, 2, 3, CH + 1])
        den = st.sb("den", [128, 2, 3, CH])
        num = st.sb("num", [128, 2, 3, CH])
        rc = st.sb("rc", [128, 2, 3, CH])
        yb = st.sb("yb", [128, 2, 3, CH])
        s = st.sb("s", [128, 2, 3])
        negs = st.sb("negs", [128, 2, 3])
        diff = st.sb("diff", [128, 2, 3])
        fac = st.sb("fac", [128, 2, 3])
        mx = st.sb("mx", [128, NCH, 3])
        pk = st.ps("pk", [128, 3, CH])
        pv = st.ps("pv", [128, 3, CH])
        cleared, vectors, weights, consts, expd, passed = map(
            st.sem, ("cleared", "vectors", "weights", "consts", "expd", "passed"))
        NV = 16 * 12
        loaded = [st.sem(f"loaded{h}") for h in range(2)]
        kv_stored = [st.sem(f"kv_stored{h}") for h in range(2)]
        y_stored = [st.sem(f"y_stored{h}") for h in range(2)]
        (xh_done, k_done, v_done, k_copied, v_copied, maxed, s_max, s_done, fac_done, b_done, bv_done,
         carried, scanned, den_done, num_done, ln_done, rc_done, y_done, mx_stored) = map(
            st.sem, ("xh_done", "k_done", "v_done", "k_copied", "v_copied", "maxed", "s_max", "s_done", "fac_done",
                     "b_done", "bv_done", "carried", "scanned", "den_done", "num_done", "ln_done", "rc_done",
                     "y_done", "mx_stored"))
        block = st.block()

        def chunk(n):
            return NCH - 1 - n

        def steps(engine, step):
            for n in range(4):
                step(n, n % 2, n // 2)
            with engine.Fori(2, NCH // 2 - 1) as i:
                for h in range(2):
                    step(2 * i + h, h, i)
            for n in range(NCH - 2, NCH + 2):
                step(n, n % 2, n // 2)

        def has(n, lag=0):
            return not isinstance(n, int) or 0 <= n - lag < NCH

        @block.sync
        def _(sp):
            tile_column(sp, sc, stat1[2 * pair], vectors, stat1[2 * pair + 1])
            tile_column(sp, dec, decay.rearrange("(c a) -> c a", a=1), vectors)
            tile_column(sp, eu, bonus.rearrange("(c a) -> c a", a=1), vectors)
            sp.wait_ge(cleared, 2)
            load_weight(sp, wk, wkt, weights)
            load_weight(sp, wv, wvt, weights)

            def step(n, h, t):
                if not has(n):
                    return
                wait(sp, xh_done, n - 1)
                own_wait(sp, passed)
                tile_loads(sp, xt[:, h], x1, pair, bass.ds(chunk(n) * CH, CH), loaded[h])
            steps(sp, step)
            sp.wait_ge(maxed, NCH)
            sp.dma_start(mx_d, mx[:, :, :]).then_inc(mx_stored, 16)
            sp.wait_ge(mx_stored, 16)
            for h in range(2):
                sp.wait_ge(kv_stored[h], 32 * (NCH // 2))
                sp.wait_ge(y_stored[h], 16 * (NCH // 2))

        @block.tensor
        def _(pe):
            pe.wait_ge(weights, 16 * 2 * LOADS_W)

            def step(n, h, t):
                if not has(n):
                    return
                pe.wait_ge(xh_done, n + 1)
                wait(pe, k_copied, n)
                project(nc, pk, wk, xh[:, h]).then_inc(k_done, 1)
                wait(pe, v_copied, n)
                project(nc, pv, wv, xh[:, h]).then_inc(v_done, 1)
            steps(pe, step)

        @block.scalar
        def _(act):
            act.preload_act_table_set("natural_log_exp_and_others")
            act.wait_ge(vectors, NV)
            nc.scalar.activation(dec[:, :, 0], dec[:, :, 0], ACT.Exp).then_inc(expd, 1)
            act.wait_ge(consts, 1)
            nc.scalar.activation(eu[:, :, 0], eu[:, :, 0], ACT.Exp).then_inc(expd, 1)
            act.wait_ge(expd, 1)
            nc.scalar.activation(ew[:, :, 0], dec[:, :, 0], ACT.Exp, scale=-1.0).then_inc(expd, 1)

            def step(n, h, t):
                g = 1 - h
                if has(n, 1):
                    act.wait_ge(s_done, n)
                    wait(act, carried, n - 2)
                    nc.scalar.activation(fac[:, g, :], diff[:, g, :], ACT.Exp).then_inc(fac_done, 1)
                    wait(act, den_done, n - 2)
                    wait(act, bv_done, n - 2)
                    for tile in range(3):
                        last = nc.scalar.activation(bt[:, g, tile, :], ks[:, g, tile, :], ACT.Exp, bias=negs[:, g, tile:tile + 1])
                    last.then_inc(b_done, 1)
                if has(n):
                    c = chunk(n)
                    act.wait_ge(k_done, n + 1)
                    wait(act, kv_stored[h], 32 * t)
                    nc.scalar.activation(flat(ks[:, h]), flat(pk[:, :, :]), ACT.Copy).then_inc(k_copied, 1)
                    act.wait_ge(k_copied, n + 1)
                    act.dma_start(k_d[bass.ds(c, 1)].rearrange("a p t -> (a p) t"), flat(ks[:, h])).then_inc(kv_stored[h], 16)
                if has(n, -1):
                    wait(act, v_done, n)
                    normalise(g, t + h)
                if has(n, 2):
                    act.wait_ge(den_done, n - 1)
                    wait(act, y_done, n - 3)
                    nc.scalar.activation(flat(rc[:, h]), flat(den[:, h]), ACT.Ln).then_inc(ln_done, 1)
                    act.wait_ge(ln_done, n - 1)
                    nc.scalar.activation(flat(rc[:, h]), flat(rc[:, h]), ACT.Exp, scale=-1.0).then_inc(rc_done, 1)
                if has(n):
                    act.wait_ge(v_done, n + 1)
                    wait(act, bv_done, n - 1)
                    nc.scalar.activation(flat(vs[:, h]), flat(pv[:, :, :]), ACT.Copy).then_inc(v_copied, 1)
                    act.wait_ge(v_copied, n + 1)
                    act.dma_start(v_d[bass.ds(c, 1)].rearrange("a p t -> (a p) t"), flat(vs[:, h])).then_inc(kv_stored[h], 16)

            def normalise(h, t):
                act.wait_ge(loaded[h], 64 * (t + 1))
                for tile in range(3):
                    last = nc.scalar.activation(xh[:, h, tile, :], xt[:, h, tile, :], ACT.Identity,
                                                scale=sc[:, tile, 0:1], bias=sc[:, tile, 1:2])
                last.then_inc(xh_done, 1)
            normalise(0, 0)
            steps(act, step)

        @block.gpsimd
        def _(pool):
            def step(n, h, t):
                g = 1 - h
                if has(n, 1):
                    pool.wait_ge(b_done, n)
                    pool.wait_ge(v_copied, n)
                    wait(pool, num_done, n - 2)
                    nc.gpsimd.tensor_tensor(flat(bv[:, g]), flat(bt[:, g]), flat(vs[:, g]), ALU.mult).then_inc(bv_done, 1)
                if has(n, 2):
                    pool.wait_ge(rc_done, n - 1)
                    pool.wait_ge(num_done, n - 1)
                    wait(pool, y_stored[h], 16 * (t - 1))
                    nc.gpsimd.tensor_tensor(flat(yb[:, h]), flat(num[:, h]), flat(rc[:, h]), ALU.mult).then_inc(y_done, 1)
                    pool.wait_ge(y_done, n - 1)
                    own_wait(pool, passed)
                    pool.dma_start(y_d[bass.ds(chunk(n - 2), 1)].rearrange("a p t -> (a p) t"), flat(yb[:, h])).then_inc(y_stored[h], 16)
            steps(pool, step)

        @block.vector
        def _(dve):
            nc.vector.memset(wk[:, :], 0.0).then_inc(cleared, 1)
            nc.vector.memset(wv[:, :], 0.0).then_inc(cleared, 1)
            nc.vector.memset(s[:, 1, :], -1e30)
            dve.wait_ge(vectors, NV)
            nc.vector.tensor_scalar(eu[:, :, 0], eu[:, :, 0], 80.0, None, ALU.min).then_inc(consts, 1)
            dve.wait_ge(expd, 3)

            def step(n, h, t):
                g = 1 - h
                if has(n, 1):
                    dve.wait_ge(k_copied, n)
                    own_wait(dve, passed)
                    m = mx[:, bass.ds(chunk(n - 1), 1), :].rearrange("p a t -> p (a t)")
                    nc.vector.tensor_reduce(m, ks[:, g], AX.X, ALU.max).then_inc(maxed, 1)
                    dve.wait_ge(maxed, n)
                    wait(dve, s_done, n - 1)
                    nc.vector.tensor_tensor(s[:, g, :], s[:, h, :], m, ALU.max).then_inc(s_max, 1)
                    dve.wait_ge(s_max, n)
                    wait(dve, b_done, n - 2)
                    nc.vector.tensor_scalar(negs[:, g, :], s[:, g, :], -1.0, None, ALU.mult)
                    nc.vector.tensor_tensor(diff[:, g, :], s[:, h, :], s[:, g, :], ALU.subtract).then_inc(s_done, 1)
                if has(n, 2):
                    recur(n - 2, h)

            def recur(m, h):
                g = 1 - h
                dve.wait_ge(fac_done, m + 1)
                if isinstance(m, int) and m == 0:
                    nc.vector.memset(qq[:, h, :, CH:CH + 1], 0.0)
                    nc.vector.memset(pp[:, h, :, CH:CH + 1], 0.0).then_inc(carried, 1)
                else:
                    dve.wait_ge(scanned, m)
                    nc.vector.tensor_tensor(qq[:, h, :, CH], qq[:, g, :, 0], fac[:, h, :], ALU.mult)
                    nc.vector.tensor_tensor(pp[:, h, :, CH], pp[:, g, :, 0], fac[:, h, :], ALU.mult).then_inc(carried, 1)
                dve.wait_ge(carried, m + 1)
                dve.wait_ge(bv_done, m + 1)
                for sums, term in ((qq, bt), (pp, bv)):
                    for tile in range(3):
                        last = nc.vector.tensor_tensor_scan(sums[:, h, tile, CH - 1::-1], ew[:, tile, :].to_broadcast([128, CH]),
                                                            term[:, h, tile, CH - 1::-1], sums[:, h, tile, CH:CH + 1],
                                                            ALU.mult, ALU.add)
                last.then_inc(scanned, 1)
                dve.wait_ge(scanned, m + 1)
                wait(dve, ln_done, m - 1)
                for tile in range(3):
                    last = nc.vector.scalar_tensor_tensor(den[:, h, tile, :], bt[:, h, tile, :], eu[:, tile, :],
                                                          qq[:, h, tile, 1:CH + 1], ALU.mult, ALU.add)
                last.then_inc(den_done, 1)
                wait(dve, y_done, m - 1)
                for tile in range(3):
                    last = nc.vector.scalar_tensor_tensor(num[:, h, tile, :], bv[:, h, tile, :], eu[:, tile, :],
                                                          pp[:, h, tile, 1:CH + 1], ALU.mult, ALU.add)
                last.then_inc(num_done, 1)
            steps(dve, step)


def wkv_forward(nc, pair, x1, stat1, wrt, wot, decay, bonus, ln_g, ln_b, k_d, v_d, y_d, mx_d, out):
    with Stage(nc, f"wf{pair}") as st:
        wr = st.sb("wr", [128, WN])
        wo = st.sb("wo", [128, WN])
        one = st.sb("one", [128, LO])
        oneb = st.sb("oneb", [128, LO])
        sc = st.sb("sc", [128, 3, 2])
        dec = st.sb("dec", [128, 3, 1])
        ew = st.sb("ew", [128, 3, 1])
        eu = st.sb("eu", [128, 3, 1])
        lg = st.sb("lg", [128, 3, 1])
        lb = st.sb("lb", [128, 3, 1])
        cb = st.sb("cb", [128, 2])
        eps = st.sb("eps", [128, 1])
        onev = st.sb("onev", [128, 1])
        xt = st.sb("xt", [128, 2, 3, CH])
        xr = st.sb("xr", [128, 2, 3, CH])
        xh = st.sb("xh", [128, 2, 3, CH])
        ks = st.sb("ks", [128, 2, 3, CH])
        vs = st.sb("vs", [128, 2, 3, CH])
        yb = st.sb("yb", [128, 2, 3, CH])
        sg = st.sb("sg", [128, 2, 3, CH])
        bt = st.sb("bt", [128, 2, 3, CH])
        bv = st.sb("bv", [128, 2, 3, CH])
        qq = st.sb("qq", [128, 2, 3, CH + 1])
        pp = st.sb("pp", [128, 2, 3, CH + 1])
        num = st.sb("num", [128, 2, 3, CH])
        hh = st.sb("hh", [128, 2, 3, CH])
        den = st.sb("den", [128, 3, CH])
        rc = st.sb("rc", [128, 3, CH])
        hsq = st.sb("hsq", [128, 3, CH])
        ot = st.sb("ot", [128, 3, CH])
        msq = st.sb("msq", [128, CH])
        var = st.sb("var", [128, CH])
        lv = st.sb("lv", [128, CH])
        ra = st.sb("ra", [128, CH])
        rb = st.sb("rb", [128, CH])
        s = st.sb("s", [128, 2, 3])
        negs = st.sb("negs", [128, 2, 3])
        diff = st.sb("diff", [128, 2, 3])
        fac = st.sb("fac", [128, 2, 3])
        mx = st.sb("mx", [128, NCH, 3])
        pr = st.ps("pr", [128, 3, CH])
        po = st.ps("po", [128, 3, CH])
        pm = st.ps("pm", [128, CH])
        pq = st.ps("pq", [128, CH])
        cleared, ones_made, vectors, weights, consts, expd, folded, means, passed = map(
            st.sem, ("cleared", "ones_made", "vectors", "weights", "consts", "expd", "folded", "means", "passed"))
        x_loaded, k_loaded, v_loaded, y_loaded, r_loaded, stored = (
            [st.sem(f"{name}{h}") for h in range(2)]
            for name in ("x_loaded", "k_loaded", "v_loaded", "y_loaded", "r_loaded", "stored"))
        (xh_done, r_done, er_done, cl_done, sg_done, s_max, s_done, fac_done, b_done, bv_done, carried, q_done,
         scanned, den_done, num_done, ln_done, rc_done, yf_done, hs_done, h_done, hsq_done, st_done, o_done,
         msq_done, var_done, lv_done, rs_done, mean_done, ot_done, out_done, lsg_done) = map(
            st.sem, ("xh_done", "r_done", "er_done", "cl_done", "sg_done", "s_max", "s_done", "fac_done", "b_done",
                     "bv_done", "carried", "q_done", "scanned", "den_done", "num_done", "ln_done", "rc_done",
                     "yf_done", "hs_done", "h_done", "hsq_done", "st_done", "o_done", "msq_done", "var_done",
                     "lv_done", "rs_done", "mean_done", "ot_done", "out_done", "lsg_done"))
        NV = 16 * (4 * 5 + 1)
        block = st.block()

        def steps(engine, step):
            for n in range(6):
                step(n, n % 2, n // 2)
            with engine.Fori(3, NCH // 2) as i:
                for h in range(2):
                    step(2 * i + h, h, i)
            for n in range(NCH, NCH + 4):
                step(n, n % 2, n // 2)

        def has(n, lag=0):
            return not isinstance(n, int) or 0 <= n - lag < NCH

        @block.sync
        def _(sp):
            tile_column(sp, sc, stat1[2 * pair], vectors, stat1[2 * pair + 1])
            for dst, src in ((dec, decay), (eu, bonus), (lg, ln_g), (lb, ln_b)):
                tile_column(sp, dst, src.rearrange("(c a) -> c a", a=1), vectors)
            sp.dma_start(mx[:, :, :], mx_d).then_inc(vectors, 16)
            sp.wait_ge(cleared, 2)
            load_weight(sp, wr, wrt, weights)
            load_weight(sp, wo, wot, weights)

            def step(n, h, t):
                if has(n):
                    wait(sp, xh_done, n - 1)
                    own_wait(sp, passed)
                    tile_loads(sp, xt[:, h], x1, pair, bass.ds(n * CH, CH), x_loaded[h])
                    wait(sp, b_done, n - 1)
                    own_wait(sp, passed)
                    sp.dma_start(flat(ks[:, h]), k_d[bass.ds(n, 1)].rearrange("a p t -> (a p) t")).then_inc(k_loaded[h], 16)
                    wait(sp, bv_done, n - 1)
                    own_wait(sp, passed)
                    sp.dma_start(flat(vs[:, h]), v_d[bass.ds(n, 1)].rearrange("a p t -> (a p) t")).then_inc(v_loaded[h], 16)
                g = 1 - h
                if has(n, 1):
                    wait(sp, hs_done, n - 2)
                    own_wait(sp, passed)
                    sp.dma_start(flat(yb[:, g]), y_d[bass.ds(n - 1, 1)].rearrange("a p t -> (a p) t")).then_inc(y_loaded[g], 16)
                if has(n, 2):
                    wait(sp, stored[h], 64 * (t - 1))
                    own_wait(sp, passed)
                    tile_loads(sp, xr[:, h], x1, pair, bass.ds((n - 2) * CH, CH), r_loaded[h])
            steps(sp, step)
            for h in range(2):
                sp.wait_ge(stored[h], 64 * (NCH // 2))

        @block.tensor
        def _(pe):
            mm = nc.tensor.matmul
            pe.wait_ge(vectors, NV)
            pe.wait_ge(weights, 16 * 2 * LOADS_W)
            mm(pm[:, 0:1], wo[:, WA1:WA1 + LO], lb[:, 0, :], start=True, stop=False)
            mm(pm[:, 0:1], wo[:, WA2:WA2 + LO], lb[:, 1, :], start=False, stop=True)
            for p in (0, 64):
                mm(pm[p:p + 64, 1:2], wo[:, WB1:WB1 + 64], lb[:, 0, :], start=True, stop=False)
                last = mm(pm[p:p + 64, 1:2], wo[:, WB2:WB2 + 64], lb[:, 1, :], start=False, stop=True)
            last.then_inc(means, 1)
            pe.wait_ge(folded, 5)
            pe.wait_ge(ones_made, 3)
            mm(pq[:, 0:LO], one[:, :], wo[:, WA1:WA1 + LO], start=True, stop=False)
            mm(pq[:, 0:LO], one[:, :], wo[:, WA2:WA2 + LO], start=False, stop=True)
            mm(pq[:, LO:LO + 64], one[:, :], wo[:, WB1:WB1 + 64], start=True, stop=False)
            mm(pq[:, LO:LO + 64], one[:, :], wo[:, WB2:WB2 + 64], start=False, stop=True).then_inc(means, 1)
            pe.wait_ge(folded, 11)

            def average(out, src):
                mm(out[:, :], oneb[:, :], src[:, 1, :], start=True, stop=False, skip_group_check=True)
                mm(out[0:64, :], one[:, 0:64], src[:, 0, :], start=False, stop=True, skip_group_check=True)
                return mm(out[64:128, :], one[:, 0:64], src[:, 2, :], start=False, stop=True, skip_group_check=True)

            def step(n, h, t):
                if has(n):
                    pe.wait_ge(xh_done, n + 1)
                    wait(pe, er_done, n)
                    project(nc, pr, wr, xh[:, h]).then_inc(r_done, 1)
                if has(n, 2):
                    pe.wait_ge(h_done, n - 1)
                    wait(pe, msq_done, n - 2)
                    average(pm, hh[:, h]).then_inc(mean_done, 1)
                    pe.wait_ge(hsq_done, n - 1)
                    wait(pe, var_done, n - 2)
                    average(pq, hsq).then_inc(st_done, 1)
                    wait(pe, ot_done, n - 2)
                    project(nc, po, wo, hh[:, h]).then_inc(o_done, 1)
            steps(pe, step)

        @block.scalar
        def _(act):
            act.preload_act_table_set("natural_log_exp_and_others")
            act.wait_ge(vectors, NV)
            nc.scalar.activation(dec[:, :, 0], dec[:, :, 0], ACT.Exp).then_inc(expd, 1)
            act.wait_ge(consts, 2)
            nc.scalar.activation(eu[:, :, 0], eu[:, :, 0], ACT.Exp).then_inc(expd, 1)
            act.wait_ge(expd, 1)
            nc.scalar.activation(ew[:, :, 0], dec[:, :, 0], ACT.Exp, scale=-1.0).then_inc(expd, 1)

            def step(n, h, t):
                g = 1 - h
                if has(n, 1):
                    act.wait_ge(r_done, n)
                    wait(act, h_done, n - 2)
                    nc.scalar.activation(flat(sg[:, g]), flat(pr[:, :, :]), ACT.Exp, scale=-1.0).then_inc(er_done, 1)
                if has(n):
                    act.wait_ge(x_loaded[h], 64 * (t + 1))
                    wait(act, r_done, n - 1)
                    for tile in range(3):
                        last = nc.scalar.activation(xh[:, h, tile, :], xt[:, h, tile, :], ACT.Identity,
                                                    scale=sc[:, tile, 0:1], bias=sc[:, tile, 1:2])
                    last.then_inc(xh_done, 1)
                    act.wait_ge(s_done, n + 1)
                    wait(act, carried, n - 1)
                    nc.scalar.activation(fac[:, h, :], diff[:, h, :], ACT.Exp).then_inc(fac_done, 1)
                    act.wait_ge(k_loaded[h], 16 * (t + 1))
                    wait(act, den_done, n - 1)
                    for tile in range(3):
                        last = nc.scalar.activation(bt[:, h, tile, :], ks[:, h, tile, :], ACT.Exp, bias=negs[:, h, tile:tile + 1])
                    last.then_inc(b_done, 1)
                if has(n, 4):
                    act.wait_ge(out_done, n - 3)
                    tok = bass.ds((n - 4) * CH, CH)
                    b0, b1 = 2 * pair, 2 * pair + 1
                    for dst, src in ((out[b0, 0:LO, tok], xr[:, h, 0, :]), (out[b1, 0:LO, tok], xr[:, h, 2, :]),
                                     (out[b0, LO:C, tok], xr[0:64, h, 1, :]), (out[b1, LO:C, tok], xr[64:128, h, 1, :])):
                        act.dma_start(dst, src).then_inc(stored[h], 16)
                if has(n, 1):
                    act.wait_ge(den_done, n)
                    wait(act, yf_done, n - 1)
                    nc.scalar.activation(flat(rc[:, :, :]), flat(den[:, :, :]), ACT.Ln).then_inc(ln_done, 1)
                    act.wait_ge(ln_done, n)
                    nc.scalar.activation(flat(rc[:, :, :]), flat(rc[:, :, :]), ACT.Exp, scale=-1.0).then_inc(rc_done, 1)
                if has(n, 3):
                    act.wait_ge(var_done, n - 2)
                    nc.scalar.activation(lv[:, :], var[:, :], ACT.Ln, bias=eps[:, 0:1]).then_inc(lv_done, 1)
                    act.wait_ge(lv_done, n - 2)
                    wait(act, ot_done, n - 3)
                    for dst, lo in ((ra, 0), (rb, 64)):
                        for p in (0, 64):
                            last = nc.scalar.activation(dst[p:p + 64, :], lv[lo:lo + 64, :], ACT.Exp, scale=-0.5)
                    last.then_inc(rs_done, 1)
                if has(n, 1):
                    act.wait_ge(cl_done, n)
                    nc.scalar.activation(flat(sg[:, g]), flat(sg[:, g]), ACT.Ln, bias=onev[:, 0:1]).then_inc(lsg_done, 1)
                    act.wait_ge(lsg_done, n)
                    nc.scalar.activation(flat(sg[:, g]), flat(sg[:, g]), ACT.Exp, scale=-1.0).then_inc(sg_done, 1)
                if has(n, 2):
                    act.wait_ge(h_done, n - 1)
                    wait(act, st_done, n - 2)
                    nc.scalar.activation(flat(hsq[:, :, :]), flat(hh[:, h]), ACT.Square).then_inc(hsq_done, 1)
                    act.wait_ge(mean_done, n - 1)
                    wait(act, var_done, n - 2)
                    nc.scalar.activation(msq[:, :], pm[:, :], ACT.Square).then_inc(msq_done, 1)
            act.wait_ge(ones_made, 3)
            steps(act, step)

        @block.gpsimd
        def _(pool):
            nc.gpsimd.memset(one[:, :], 1.0 / C)
            nc.gpsimd.memset(oneb[:, :], 0.0)
            nc.gpsimd.memset(eps[:, :], 4 * LN_EPS)
            nc.gpsimd.memset(onev[:, :], 1.0).then_inc(ones_made, 1)
            for k in range(2):
                pool.wait_ge(ones_made, k + 1)
                nc.gpsimd.memset(oneb[64 * k:64 * k + 64, 64 * k:64 * k + 64], 1.0 / C).then_inc(ones_made, 1)

            def step(n, h, t):
                g = 1 - h
                if has(n):
                    pool.wait_ge(b_done, n + 1)
                    pool.wait_ge(v_loaded[h], 16 * (t + 1))
                    wait(pool, num_done, n - 1)
                    nc.gpsimd.tensor_tensor(flat(bv[:, h]), flat(bt[:, h]), flat(vs[:, h]), ALU.mult).then_inc(bv_done, 1)
                if has(n, 1):
                    pool.wait_ge(rc_done, n)
                    pool.wait_ge(num_done, n)
                    nc.gpsimd.tensor_tensor(flat(num[:, g]), flat(num[:, g]), flat(rc[:, :, :]), ALU.mult).then_inc(yf_done, 1)
                    pool.wait_ge(yf_done, n)
                    pool.wait_ge(y_loaded[g], 16 * (t + h))
                    nc.gpsimd.tensor_tensor(flat(num[:, g]), flat(num[:, g]), flat(yb[:, g]), ALU.add).then_inc(hs_done, 1)
            steps(pool, step)

        @block.vector
        def _(dve):
            nc.vector.memset(wr[:, :], 0.0).then_inc(cleared, 1)
            nc.vector.memset(wo[:, :], 0.0).then_inc(cleared, 1)
            nc.vector.memset(s[:, 1, :], -1e30)
            dve.wait_ge(vectors, NV)
            nc.vector.tensor_scalar(eu[:, :, 0], eu[:, :, 0], 80.0, None, ALU.min).then_inc(consts, 2)
            dve.wait_ge(means, 1)
            nc.vector.tensor_copy(cb[:, :], pm[:, 0:2])
            for at, n, tile in ((WA1, LO, 0), (WB1, 64, 0), (WA2, LO, 1), (WC2, LO, 1), (WB2, LO, 1)):
                nc.vector.tensor_scalar(wo[:, at:at + n], wo[:, at:at + n], lg[:, tile, :], None, ALU.mult).then_inc(folded, 1)
            dve.wait_ge(means, 2)
            dve.wait_ge(folded, 5)
            for lo, hi, at, n, m in ((0, 128, WA1, LO, 0), (0, 64, WA2, LO, 0), (64, 128, WC2, LO, 0),
                                     (0, 128, WB1, 64, LO), (0, 64, WB2, 64, LO), (64, 128, WB2 + 64, 64, LO)):
                nc.vector.tensor_tensor(wo[lo:hi, at:at + n], wo[lo:hi, at:at + n], pq[lo:hi, m:m + n],
                                        ALU.subtract).then_inc(folded, 1)
            dve.wait_ge(expd, 3)

            def step(n, h, t):
                g = 1 - h
                if has(n):
                    m = mx[:, bass.ds(n, 1), :].rearrange("p a t -> p (a t)")
                    wait(dve, s_done, n)
                    nc.vector.tensor_tensor(s[:, h, :], s[:, g, :], m, ALU.max).then_inc(s_max, 1)
                    dve.wait_ge(s_max, n + 1)
                    wait(dve, b_done, n - 1)
                    nc.vector.tensor_scalar(negs[:, h, :], s[:, h, :], -1.0, None, ALU.mult)
                    nc.vector.tensor_tensor(diff[:, h, :], s[:, g, :], s[:, h, :], ALU.subtract).then_inc(s_done, 1)
                if has(n, 1):
                    dve.wait_ge(er_done, n)
                    nc.vector.tensor_scalar(flat(sg[:, g]), flat(sg[:, g]), 2.0 ** 60, None, ALU.min).then_inc(cl_done, 1)
                    carry(n - 1, g)
                    scans(g, qq, bt).then_inc(q_done, 1)
                if has(n, 1):
                    dve.wait_ge(q_done, n)
                    wait(dve, ln_done, n - 1)
                    for tile in range(3):
                        last = nc.vector.scalar_tensor_tensor(den[:, tile, :], bt[:, g, tile, :], eu[:, tile, :],
                                                              qq[:, g, tile, 0:CH], ALU.mult, ALU.add)
                    last.then_inc(den_done, 1)
                if has(n, 3):
                    dve.wait_ge(msq_done, n - 2)
                    dve.wait_ge(st_done, n - 2)
                    wait(dve, lv_done, n - 3)
                    nc.vector.tensor_tensor(var[:, :], pq[:, :], msq[:, :], ALU.subtract).then_inc(var_done, 1)
                if has(n, 1):
                    dve.wait_ge(bv_done, n)
                    scans(g, pp, bv).then_inc(scanned, 1)
                    dve.wait_ge(scanned, n)
                    for tile in range(3):
                        last = nc.vector.scalar_tensor_tensor(num[:, g, tile, :], bv[:, g, tile, :], eu[:, tile, :],
                                                              pp[:, g, tile, 0:CH], ALU.mult, ALU.add)
                    last.then_inc(num_done, 1)
                if has(n, 2):
                    dve.wait_ge(hs_done, n - 1)
                    dve.wait_ge(sg_done, n - 1)
                    wait(dve, o_done, n - 3)
                    nc.vector.tensor_tensor(flat(hh[:, h]), flat(num[:, h]), flat(sg[:, h]), ALU.mult).then_inc(h_done, 1)
                if has(n, 3):
                    finish(n - 3, g, t)

            def carry(m, h):
                g = 1 - h
                dve.wait_ge(fac_done, m + 1)
                if isinstance(m, int) and m == 0:
                    nc.vector.memset(qq[:, h, :, 0:1], 0.0)
                    nc.vector.memset(pp[:, h, :, 0:1], 0.0).then_inc(carried, 1)
                else:
                    dve.wait_ge(scanned, m)
                    nc.vector.tensor_tensor(qq[:, h, :, 0], qq[:, g, :, CH], fac[:, h, :], ALU.mult)
                    nc.vector.tensor_tensor(pp[:, h, :, 0], pp[:, g, :, CH], fac[:, h, :], ALU.mult).then_inc(carried, 1)
                dve.wait_ge(carried, m + 1)
                dve.wait_ge(b_done, m + 1)

            def scans(h, sums, term):
                for tile in range(3):
                    last = nc.vector.tensor_tensor_scan(sums[:, h, tile, 1:CH + 1], ew[:, tile, :].to_broadcast([128, CH]),
                                                        term[:, h, tile, :], sums[:, h, tile, 0:1], ALU.mult, ALU.add)
                return last

            def finish(m, h, t):
                dve.wait_ge(rs_done, m + 1)
                dve.wait_ge(o_done, m + 1)
                nc.vector.tensor_tensor(ot[:, 0, :], po[:, 0, :], ra[:, :], ALU.mult)
                nc.vector.tensor_tensor(ot[:, 2, :], po[:, 2, :], rb[:, :], ALU.mult)
                nc.vector.tensor_tensor(ot[0:64, 1, :], po[0:64, 1, :], ra[0:64, :], ALU.mult)
                nc.vector.tensor_tensor(ot[64:128, 1, :], po[64:128, 1, :], rb[64:128, :], ALU.mult).then_inc(ot_done, 1)
                dve.wait_ge(ot_done, m + 1)
                dve.wait_ge(r_loaded[h], 64 * (t - 1 if h == 1 else t))
                for tile in range(3):
                    last = nc.vector.scalar_tensor_tensor(xr[:, h, tile, :], ot[:, tile, :], cb[:, tile % 2:tile % 2 + 1],
                                                          xr[:, h, tile, :], ALU.add, ALU.add)
                last.then_inc(out_done, 1)
            steps(dve, step)


def build(nc, io, out):
    def scratch(name, shape):
        return nc.dram_tensor(name, shape, F).ap()

    stat0 = scratch("stat0", (B * GROUPS, 2))
    u = scratch("u", (C3, B, HW))
    gate_sums = scratch("gate_sums", (1, B * HW // 512))
    bands = scratch("bands", (2 * C * 3, 256))
    d = scratch("d", (B, PAD_IMG))
    gram_d = scratch("gram_d", (2 * CPG, B * HEADS, 2 * CPG))
    attn_d = scratch("attn_d", (CPG, B * HEADS, CPG))
    rank_d = scratch("rank_d", (CPG, B * HEADS, CPG))
    flags = scratch("flags", (48, W + 2, CPG))
    t = scratch("t", (B, C, H, W))
    pt_d = scratch("pt_d", (B, C, C))
    x1 = scratch("x1", (B, C, HW))
    stat1 = scratch("stat1", (B, C, 2))
    k_d = scratch("k_d", (NCH, 128, 3 * CH))
    v_d = scratch("v_d", (NCH, 128, 3 * CH))
    y_d = scratch("y_d", (NCH, 128, 3 * CH))
    mx_d = scratch("mx_d", (128, NCH, 3))
    x = io["x"]
    group_stats(nc, x, stat0)
    pointwise(nc, x, stat0, io["w1t"], io["gate_b1"], io["gate_w2t"], io["gate_b2"], u, gate_sums)
    depthwise(nc, u, io["qkv_dw_w"], bands, d)
    gram(nc, d, gram_d)
    attention_scores(nc, gram_d, io["temperature"], attn_d)
    branch_conv(nc, x, d, io["fcb"], io["branch_w"], io["branch_b"], flags, attn_d, rank_d, t)
    attention_weights(nc, attn_d, rank_d, gate_sums, io["projt"], pt_d)
    apply_attention(nc, d, t, pt_d, x1, stat1)
    o = out.rearrange("b c h w -> b c (h w)")
    for pair in range(B // 2):
        wkv_backward(nc, pair, x1, stat1, io["wkt"], io["wvt"], io["w_decay"], io["u"], k_d, v_d, y_d, mx_d)
        wkv_forward(nc, pair, x1, stat1, io["wrt"], io["wot"], io["w_decay"], io["u"], io["ln_g"], io["ln_b"],
                    k_d, v_d, y_d, mx_d, o)


def kernel(**inputs):
    import numpy as np
    import concourse.bacc as bacc
    from concourse.bass_utils import run_bass_kernel_spmd

    def f(name):
        return np.asarray(inputs[name])

    qkv_w = f("L0_conv_qkv_w").reshape(C3, C)
    gate_w1 = f("L0_conv_gate_w1").reshape(HALF, C)
    fc_w = f("L0_conv_fc_w").reshape(9, G3)
    arrays = {
        "x": f("x"),
        "w1t": np.concatenate([gate_w1.T, qkv_w.T], axis=1),
        "gate_b1": f("L0_conv_gate_b1"),
        "gate_w2t": f("L0_conv_gate_w2").reshape(1, HALF).T,
        "gate_b2": f("L0_conv_gate_b2"),
        "qkv_dw_w": f("L0_conv_qkv_dw_w"),
        "temperature": f("L0_conv_temperature"),
        "projt": f("L0_conv_proj_w").reshape(C, C).T,
        "fcb": np.concatenate([fc_w, f("L0_conv_fc_b").reshape(9, 1)], axis=1),
        "branch_w": f("L0_conv_dep_w"),
        "branch_b": f("L0_conv_dep_b"),
        "wkt": f("L1_conv_Wk").T,
        "wvt": f("L1_conv_Wv").T,
        "wrt": f("L1_conv_Wr").T,
        "wot": f("L1_conv_Wo").T,
        "w_decay": f("L1_conv_w_decay"),
        "u": f("L1_conv_u"),
        "ln_g": f("L1_conv_ln_g"),
        "ln_b": f("L1_conv_ln_b"),
    }
    nc = bacc.Bacc("TRN2", target_bir_lowering=False, num_devices=1)
    maps, io = {}, {}
    for name, a in arrays.items():
        a = np.ascontiguousarray(a)
        maps[f"in_{name}"] = a
        io[name] = nc.dram_tensor(f"in_{name}", a.shape, mybir.dt.from_np(a.dtype), kind="ExternalInput").ap()
    out = nc.dram_tensor("out", (B, C, H, W), F, kind="ExternalOutput").ap()
    build(nc, io, out)
    return run_bass_kernel_spmd(nc, [maps], core_ids=[0]).results[0]["out"]
```
